# Optimizing a Trainium2 kernel written in Bass

```python
import numpy as np
import jax
import jax.numpy as jnp

def _softmax(x, axis=-1):
    return jax.nn.softmax(x, axis=axis)

def _gelu(x):
    return jax.nn.gelu(x, approximate=True)

def _silu(x):
    return jax.nn.silu(x)

def _sigmoid(x):
    return jax.nn.sigmoid(x)

def _layernorm(x, axis=-1, eps=1e-05):
    m = jnp.mean(x, axis=axis, keepdims=True)
    v = jnp.var(x, axis=axis, keepdims=True)
    return (x - m) / jnp.sqrt(v + eps)

def _scatter_add(tgt, idx, src, axis=0):
    return tgt.at[idx].add(src)

def _segment_sum(src, seg, n):
    return jax.ops.segment_sum(src, seg, n)
kernel_name = 'mk_xattn_seq_d2_seqx_r4_36872d'

def setup_inputs(seed: int=0):
    np.random.seed(seed)
    _w = jnp.asarray

    def _rec_inputs():
        import jax
        import jax.numpy as jnp
        _rk = jax.random.key(seed)
        x = -0.0002928 + 1 * jax.random.normal(jax.random.fold_in(_rk, 1), (32, 128, 256), jnp.float32)
        _lenS = 128 - jax.random.randint(jax.random.fold_in(_rk, 7), (32,), 0, max(1, 128 // 4) + 1, jnp.int32)
        _lenS2 = 128 - jax.random.randint(jax.random.fold_in(_rk, 8), (32,), 0, max(1, 128 // 4) + 1, jnp.int32)
        _ctx_768P = jax.random.normal(jax.random.fold_in(_rk, 11), (32, 16, 192), jnp.float32)
        _ctx_768c = jax.random.dirichlet(jax.random.fold_in(_rk, 511), 0.3 * jnp.ones((16,), jnp.float32), (32, 128))
        _ctx_768t = jnp.einsum('bsk,bkd->bsd', _ctx_768c, _ctx_768P)
        _ctx_768t = _ctx_768t * jax.lax.rsqrt(jnp.mean(jnp.square(_ctx_768t)) + 1e-12) * 0.953939
        ctx_768 = 2.09791e-05 + 1.00001 * (_ctx_768t + 0.3 * jax.random.normal(jax.random.fold_in(_rk, 611), (32, 128, 192), jnp.float32))
        _validS = jnp.arange(128)[None, :] < _lenS[:, None]
        _validS2 = jnp.arange(128)[None, :] < _lenS2[:, None]
        _causal = jnp.tril(jnp.ones((128, 128), dtype=bool))
        mask_BxS_bf0 = jnp.logical_not(jnp.ones((32, 128), dtype=bool))
        mask_BxS2_bf0 = jnp.logical_not(jnp.ones((32, 128), dtype=bool))
        return (x, ctx_768, mask_BxS_bf0, mask_BxS2_bf0)
    x, ctx_768, mask_BxS_bf0, mask_BxS2_bf0 = _rec_inputs()

    def _L0_xattn_setup():
        import jax, jax.numpy as jnp
        import numpy as np
        D_Q, D_CTX, N_HEADS, HEAD_DIM = (256, 192, 16, 64)
        INNER = N_HEADS * HEAD_DIM
        EPS = 1e-05

        def _layernorm(x, gamma, beta):
            mu = jnp.mean(x, axis=-1, keepdims=True)
            var = jnp.var(x, axis=-1, keepdims=True)
            return (x - mu) * jax.lax.rsqrt(var + EPS) * gamma + beta
        key = jax.random.key(seed)
        ks = jax.random.split(key, 8)
        B, NQ, NC = (4, 256, 256)
        s_q = 1.0 / np.sqrt(D_Q)
        s_c = 1.0 / np.sqrt(D_CTX)
        s_i = 1.0 / np.sqrt(INNER)
        return {'x': jax.random.normal(ks[0], (B, NQ, D_Q), jnp.float32), 'context': jax.random.normal(ks[1], (B, NC, D_CTX), jnp.float32), 'Wq': jax.random.normal(ks[2], (D_Q, INNER), jnp.float32) * s_q, 'Wk': jax.random.normal(ks[3], (D_CTX, INNER), jnp.float32) * s_c, 'Wv': jax.random.normal(ks[4], (D_CTX, INNER), jnp.float32) * s_c, 'Wo': jax.random.normal(ks[5], (INNER, D_Q), jnp.float32) * s_i, 'bo': jnp.zeros((D_Q,), jnp.float32), 'gamma': jnp.ones((D_Q,), jnp.float32), 'beta': jnp.zeros((D_Q,), jnp.float32)}
    _L0_xattn_all = _L0_xattn_setup()
    _L0_xattn_in = {k: v for k, v in _L0_xattn_all.items() if k in ('Wq', 'Wk', 'Wv', 'Wo', 'bo', 'gamma', 'beta')}
    del _L0_xattn_all

    def _L1_xattn_setup():
        import jax, jax.numpy as jnp
        import numpy as np
        D_DEC, D_ENC, H, D_MLP = (256, 192, 16, 1024)
        HD = D_DEC // H

        def _layernorm(x, w, b, eps=1e-05):
            m = x.mean(-1, keepdims=True)
            v = ((x - m) ** 2).mean(-1, keepdims=True)
            return (x - m) / jnp.sqrt(v + eps) * w + b

        def _decoder_block(x, enc, tgt_mask, enc_mask, ln1_w, ln1_b, qkv_w, qkv_b, proj_w, proj_b, ln2_w, ln2_b, q_w, q_b, k_w, k_b, v_w, v_b, out_w, out_b, ln3_w, ln3_b, mlp1_w, mlp1_b, mlp2_w, mlp2_b):
            B, T, C = x.shape
            S = enc.shape[1]
            scale = HD ** (-0.5)
            neg = jnp.asarray(-jnp.inf, x.dtype)
            h = _layernorm(x, ln1_w, ln1_b)
            qkv = (h @ qkv_w + qkv_b).reshape(B, T, 3, H, HD)
            q, k, v = [qkv[:, :, i].transpose(0, 2, 1, 3) for i in range(3)]
            attn = jnp.einsum('bhtd,bhsd->bhts', q, k) * scale
            causal = jnp.triu(jnp.ones((T, T), bool), 1)
            attn = jnp.where(causal[None, None], neg, attn)
            attn = jnp.where(tgt_mask[:, None, None, :], neg, attn)
            attn = jax.nn.softmax(attn, axis=-1)
            sa = jnp.einsum('bhts,bhsd->bhtd', attn, v).transpose(0, 2, 1, 3).reshape(B, T, C)
            x = x + sa @ proj_w + proj_b
            h = _layernorm(x, ln2_w, ln2_b)
            q = (h @ q_w + q_b).reshape(B, T, H, HD).transpose(0, 2, 1, 3)
            k = (enc @ k_w + k_b).reshape(B, S, H, HD).transpose(0, 2, 1, 3)
            v = (enc @ v_w + v_b).reshape(B, S, H, HD).transpose(0, 2, 1, 3)
            attn = jnp.einsum('bhtd,bhsd->bhts', q, k) * scale
            attn = jnp.where(enc_mask[:, None, None, :], neg, attn)
            attn = jax.nn.softmax(attn, axis=-1)
            ca = jnp.einsum('bhts,bhsd->bhtd', attn, v).transpose(0, 2, 1, 3).reshape(B, T, C)
            x = x + ca @ out_w + out_b
            h = _layernorm(x, ln3_w, ln3_b)
            h = jax.nn.gelu(h @ mlp1_w + mlp1_b, approximate=False)
            x = x + h @ mlp2_w + mlp2_b
            return x
        key = jax.random.key(seed)
        ks = jax.random.split(key, 16)
        B, T, S = (4, 256, 144)

        def lin(k, din, dout):
            kw, kb = jax.random.split(k)
            bound = 1.0 / np.sqrt(din)
            W = jax.random.uniform(kw, (din, dout), jnp.float32, -bound, bound)
            b = jax.random.uniform(kb, (dout,), jnp.float32, -bound, bound)
            return (W, b)
        qkv_w, qkv_b = lin(ks[0], D_DEC, 3 * D_DEC)
        proj_w, proj_b = lin(ks[1], D_DEC, D_DEC)
        q_w, q_b = lin(ks[2], D_DEC, D_DEC)
        k_w, k_b = lin(ks[3], D_ENC, D_DEC)
        v_w, v_b = lin(ks[4], D_ENC, D_DEC)
        out_w, out_b = lin(ks[5], D_DEC, D_DEC)
        mlp1_w, mlp1_b = lin(ks[6], D_DEC, D_MLP)
        mlp2_w, mlp2_b = lin(ks[7], D_MLP, D_DEC)
        return {'x': jax.random.normal(ks[8], (B, T, D_DEC), jnp.float32), 'enc': jax.random.normal(ks[9], (B, S, D_ENC), jnp.float32), 'tgt_key_padding_mask': jnp.zeros((B, T), bool), 'enc_padding_mask': jnp.zeros((B, S), bool), 'ln1_w': jnp.ones((D_DEC,)), 'ln1_b': jnp.zeros((D_DEC,)), 'qkv_w': qkv_w, 'qkv_b': qkv_b, 'proj_w': proj_w, 'proj_b': proj_b, 'ln2_w': jnp.ones((D_DEC,)), 'ln2_b': jnp.zeros((D_DEC,)), 'q_w': q_w, 'q_b': q_b, 'k_w': k_w, 'k_b': k_b, 'v_w': v_w, 'v_b': v_b, 'out_w': out_w, 'out_b': out_b, 'ln3_w': jnp.ones((D_DEC,)), 'ln3_b': jnp.zeros((D_DEC,)), 'mlp1_w': mlp1_w, 'mlp1_b': mlp1_b, 'mlp2_w': mlp2_w, 'mlp2_b': mlp2_b}
    _L1_xattn_all = _L1_xattn_setup()
    _L1_xattn_in = {k: v for k, v in _L1_xattn_all.items() if k in ('ln1_w', 'ln1_b', 'qkv_w', 'qkv_b', 'proj_w', 'proj_b', 'ln2_w', 'ln2_b', 'q_w', 'q_b', 'k_w', 'k_b', 'v_w', 'v_b', 'out_w', 'out_b', 'ln3_w', 'ln3_b', 'mlp1_w', 'mlp1_b', 'mlp2_w', 'mlp2_b')}
    del _L1_xattn_all
    return {'x': x, 'ctx_768': ctx_768, 'mask_BxS_bf0': mask_BxS_bf0, 'mask_BxS2_bf0': mask_BxS2_bf0, 'L0_xattn_Wq': _L0_xattn_in['Wq'], 'L0_xattn_Wk': _L0_xattn_in['Wk'], 'L0_xattn_Wv': _L0_xattn_in['Wv'], 'L0_xattn_Wo': _L0_xattn_in['Wo'], 'L0_xattn_bo': _L0_xattn_in['bo'], 'L0_xattn_gamma': _L0_xattn_in['gamma'], 'L0_xattn_beta': _L0_xattn_in['beta'], 'L1_xattn_ln1_w': _L1_xattn_in['ln1_w'], 'L1_xattn_ln1_b': _L1_xattn_in['ln1_b'], 'L1_xattn_qkv_w': _L1_xattn_in['qkv_w'], 'L1_xattn_qkv_b': _L1_xattn_in['qkv_b'], 'L1_xattn_proj_w': _L1_xattn_in['proj_w'], 'L1_xattn_proj_b': _L1_xattn_in['proj_b'], 'L1_xattn_ln2_w': _L1_xattn_in['ln2_w'], 'L1_xattn_ln2_b': _L1_xattn_in['ln2_b'], 'L1_xattn_q_w': _L1_xattn_in['q_w'], 'L1_xattn_q_b': _L1_xattn_in['q_b'], 'L1_xattn_k_w': _L1_xattn_in['k_w'], 'L1_xattn_k_b': _L1_xattn_in['k_b'], 'L1_xattn_v_w': _L1_xattn_in['v_w'], 'L1_xattn_v_b': _L1_xattn_in['v_b'], 'L1_xattn_out_w': _L1_xattn_in['out_w'], 'L1_xattn_out_b': _L1_xattn_in['out_b'], 'L1_xattn_ln3_w': _L1_xattn_in['ln3_w'], 'L1_xattn_ln3_b': _L1_xattn_in['ln3_b'], 'L1_xattn_mlp1_w': _L1_xattn_in['mlp1_w'], 'L1_xattn_mlp1_b': _L1_xattn_in['mlp1_b'], 'L1_xattn_mlp2_w': _L1_xattn_in['mlp2_w'], 'L1_xattn_mlp2_b': _L1_xattn_in['mlp2_b']}

def reference(x, ctx_768, mask_BxS_bf0, mask_BxS2_bf0, L0_xattn_Wq, L0_xattn_Wk, L0_xattn_Wv, L0_xattn_Wo, L0_xattn_bo, L0_xattn_gamma, L0_xattn_beta, L1_xattn_ln1_w, L1_xattn_ln1_b, L1_xattn_qkv_w, L1_xattn_qkv_b, L1_xattn_proj_w, L1_xattn_proj_b, L1_xattn_ln2_w, L1_xattn_ln2_b, L1_xattn_q_w, L1_xattn_q_b, L1_xattn_k_w, L1_xattn_k_b, L1_xattn_v_w, L1_xattn_v_b, L1_xattn_out_w, L1_xattn_out_b, L1_xattn_ln3_w, L1_xattn_ln3_b, L1_xattn_mlp1_w, L1_xattn_mlp1_b, L1_xattn_mlp2_w, L1_xattn_mlp2_b):
    import jax
    import jax.numpy as jnp

    def _L0_xattn_ref(x, context, Wq, Wk, Wv, Wo, bo, gamma, beta):
        import jax, jax.numpy as jnp
        import numpy as np
        D_Q, D_CTX, N_HEADS, HEAD_DIM = (256, 192, 16, 64)
        INNER = N_HEADS * HEAD_DIM
        EPS = 1e-05

        def _layernorm(x, gamma, beta):
            mu = jnp.mean(x, axis=-1, keepdims=True)
            var = jnp.var(x, axis=-1, keepdims=True)
            return (x - mu) * jax.lax.rsqrt(var + EPS) * gamma + beta
        scale = HEAD_DIM ** (-0.5)
        h = _layernorm(x, gamma, beta)
        B, NQ, _ = x.shape
        NC = context.shape[1]
        Q = (h @ Wq).reshape(B, NQ, N_HEADS, HEAD_DIM)
        K = (context @ Wk).reshape(B, NC, N_HEADS, HEAD_DIM)
        V = (context @ Wv).reshape(B, NC, N_HEADS, HEAD_DIM)
        attn = jnp.einsum('bihd,bjhd->bhij', Q, K)
        attn = jax.nn.softmax(attn, axis=-1) * scale
        vals = jnp.einsum('bhij,bjhd->bihd', attn, V).reshape(B, NQ, INNER)
        out = vals @ Wo + bo
        return x + out

    def _L1_xattn_ref(x, enc, tgt_key_padding_mask, enc_padding_mask, ln1_w, ln1_b, qkv_w, qkv_b, proj_w, proj_b, ln2_w, ln2_b, q_w, q_b, k_w, k_b, v_w, v_b, out_w, out_b, ln3_w, ln3_b, mlp1_w, mlp1_b, mlp2_w, mlp2_b):
        import jax, jax.numpy as jnp
        import numpy as np
        D_DEC, D_ENC, H, D_MLP = (256, 192, 16, 1024)
        HD = D_DEC // H

        def _layernorm(x, w, b, eps=1e-05):
            m = x.mean(-1, keepdims=True)
            v = ((x - m) ** 2).mean(-1, keepdims=True)
            return (x - m) / jnp.sqrt(v + eps) * w + b

        def _decoder_block(x, enc, tgt_mask, enc_mask, ln1_w, ln1_b, qkv_w, qkv_b, proj_w, proj_b, ln2_w, ln2_b, q_w, q_b, k_w, k_b, v_w, v_b, out_w, out_b, ln3_w, ln3_b, mlp1_w, mlp1_b, mlp2_w, mlp2_b):
            B, T, C = x.shape
            S = enc.shape[1]
            scale = HD ** (-0.5)
            neg = jnp.asarray(-jnp.inf, x.dtype)
            h = _layernorm(x, ln1_w, ln1_b)
            qkv = (h @ qkv_w + qkv_b).reshape(B, T, 3, H, HD)
            q, k, v = [qkv[:, :, i].transpose(0, 2, 1, 3) for i in range(3)]
            attn = jnp.einsum('bhtd,bhsd->bhts', q, k) * scale
            causal = jnp.triu(jnp.ones((T, T), bool), 1)
            attn = jnp.where(causal[None, None], neg, attn)
            attn = jnp.where(tgt_mask[:, None, None, :], neg, attn)
            attn = jax.nn.softmax(attn, axis=-1)
            sa = jnp.einsum('bhts,bhsd->bhtd', attn, v).transpose(0, 2, 1, 3).reshape(B, T, C)
            x = x + sa @ proj_w + proj_b
            h = _layernorm(x, ln2_w, ln2_b)
            q = (h @ q_w + q_b).reshape(B, T, H, HD).transpose(0, 2, 1, 3)
            k = (enc @ k_w + k_b).reshape(B, S, H, HD).transpose(0, 2, 1, 3)
            v = (enc @ v_w + v_b).reshape(B, S, H, HD).transpose(0, 2, 1, 3)
            attn = jnp.einsum('bhtd,bhsd->bhts', q, k) * scale
            attn = jnp.where(enc_mask[:, None, None, :], neg, attn)
            attn = jax.nn.softmax(attn, axis=-1)
            ca = jnp.einsum('bhts,bhsd->bhtd', attn, v).transpose(0, 2, 1, 3).reshape(B, T, C)
            x = x + ca @ out_w + out_b
            h = _layernorm(x, ln3_w, ln3_b)
            h = jax.nn.gelu(h @ mlp1_w + mlp1_b, approximate=False)
            x = x + h @ mlp2_w + mlp2_b
            return x
        return _decoder_block(x, enc, tgt_key_padding_mask, enc_padding_mask, ln1_w, ln1_b, qkv_w, qkv_b, proj_w, proj_b, ln2_w, ln2_b, q_w, q_b, k_w, k_b, v_w, v_b, out_w, out_b, ln3_w, ln3_b, mlp1_w, mlp1_b, mlp2_w, mlp2_b)
    x = _L0_xattn_ref(x, ctx_768, L0_xattn_Wq, L0_xattn_Wk, L0_xattn_Wv, L0_xattn_Wo, L0_xattn_bo, L0_xattn_gamma, L0_xattn_beta)
    x = _L1_xattn_ref(x, ctx_768, mask_BxS_bf0, mask_BxS2_bf0, L1_xattn_ln1_w, L1_xattn_ln1_b, L1_xattn_qkv_w, L1_xattn_qkv_b, L1_xattn_proj_w, L1_xattn_proj_b, L1_xattn_ln2_w, L1_xattn_ln2_b, L1_xattn_q_w, L1_xattn_q_b, L1_xattn_k_w, L1_xattn_k_b, L1_xattn_v_w, L1_xattn_v_b, L1_xattn_out_w, L1_xattn_out_b, L1_xattn_ln3_w, L1_xattn_ln3_b, L1_xattn_mlp1_w, L1_xattn_mlp1_b, L1_xattn_mlp2_w, L1_xattn_mlp2_b)
    return x

_drawn_inputs = setup_inputs


def setup_inputs(seed=0):
    import zlib

    import numpy as np

    out = dict(_drawn_inputs(seed))
    spreads = {'L0_xattn_bo': (0.0, 0.1),
     'L0_xattn_gamma': (1.0, 0.2),
     'L0_xattn_beta': (0.0, 0.326),
     'L1_xattn_ln1_w': (1.0, 0.6),
     'L1_xattn_ln1_b': (0.0, 0.1),
     'L1_xattn_ln2_w': (1.0, 0.6),
     'L1_xattn_ln2_b': (0.0, 2.0),
     'L1_xattn_ln3_w': (1.0, 0.2),
     'L1_xattn_ln3_b': (0.0, 0.425)}
    factors = {'L1_xattn_qkv_b': 3.085,
     'L1_xattn_q_b': 40.015,
     'L1_xattn_k_b': 64.0,
     'L1_xattn_mlp1_b': 4.431,
     'L1_xattn_mlp2_b': 3.213}
    for name, (base, spread) in spreads.items():
        noise = np.random.default_rng([zlib.crc32(name.encode()), seed]).standard_normal(out[name].shape)
        drawn = base * np.exp(spread * noise) if base else spread * noise
        out[name] = jnp.asarray(drawn.astype(out[name].dtype))
    for name, factor in factors.items():
        out[name] = (out[name] * factor).astype(out[name].dtype)
    return out
```

```python
from contextlib import ExitStack

import concourse.bass as bass
from concourse import mybir

F32 = mybir.dt.float32
F32R = mybir.dt.float32r
BF16 = mybir.dt.bfloat16
U8 = mybir.dt.uint8
ALU = mybir.AluOpType
ACT = mybir.ActivationFunctionType
AX = mybir.AxisListType.X

P = 128
PAIR = 2
EPS = 1e-5
MASKED = -3.0e38
LAG_T, LAG_PV, LAG_O = 2, 3, 4

PER = dict(
    x_loaded=16, c_loaded=16, masks_loaded=64, y_stored=32,
    ln_stats=12, ln_aggr=8, ln_var=4, ln_rstd=4, xhat_ready=8, xhatT_ready=4, h_full=8, h_hi=4, h_lo=4,
    cT_ready=1, c_hi=2, c_lo=2, masks_ready=2,
    k0_ready=4, k0_done=4, v0_ready=4, v0_done=4, q0_ready=4, q0_done=4,
    scores_ready=24, raw_max=16, nmax_ready=24, exp_done=24, pt_ready=24, pts_ready=24, pv_done=24,
    recip0=8, on_ready=12, recip1=4, oT_ready=10, oT_hi=12, oT_lo=12,
    resid_ready=5, resid_done=5, xb_ready=4,
    k1_ready=2, k1_done=4, v1_ready=2, v1_done=2, q1_ready=2, q1_done=8,
    up_ready=4, gelu_done=8, g_hi=4, g_lo=4,
)
CREDIT = dict(resid_done=1, y_stored=1)


def decoder_kernel(nc, a, out):
    B, T, D = a["x"].shape
    DC = a["ctx_768"].shape[2]
    INNER = a["L0_xattn_Wq"].shape[1]
    DM = a["L1_xattn_mlp1_w"].shape[1]
    H = 16
    HD0, HD1 = INNER // H, D // H
    TURNS = B // PAIR
    TOK = PAIR * T
    KT = D // P
    DC1 = DC - P
    T0, T1, TM = INNER // P, D // P, DM // P
    GROUPS = PAIR * H // 4
    CK = [P, DC1]

    ctx = ExitStack()
    with ctx:
        def sb(name, shape, dt=F32, stack=ctx):
            return stack.enter_context(nc.sbuf_tensor(name, shape, dt))

        S = {n: ctx.enter_context(nc.semaphore(n)) for n in PER}
        S.update({n: ctx.enter_context(nc.semaphore(n)) for n in
                  ("w_hi_done", "w_lo_done", "params_loaded", "consts_built", "prep_steps", "prepared",
                   "params_turned", "ones_set")})
        w_loaded = [ctx.enter_context(nc.semaphore(f"w_loaded{n}")) for n in range(8)]

        def at(sem, i, k):
            return i * PER[sem] + k + CREDIT.get(sem, 0)

        def split_pair(name, shape):
            return sb(name + "_hi", shape, F32R), sb(name + "_lo", shape, F32R)

        WEIGHTS = [
            ("wk", a["L0_xattn_Wk"]), ("wv", a["L0_xattn_Wv"]), ("wq", a["L0_xattn_Wq"]), ("wo", a["L0_xattn_Wo"]),
            ("qkv", a["L1_xattn_qkv_w"]), ("mid", None), ("up", a["L1_xattn_mlp1_w"]), ("down", a["L1_xattn_mlp2_w"])]
        MID = [("k2", "L1_xattn_k_w"), ("v2", "L1_xattn_v_w"), ("pr", "L1_xattn_proj_w"), ("q2", "L1_xattn_q_w"),
               ("ou", "L1_xattn_out_w")]
        W = {}
        W["wk"] = split_pair("wk", [P, 2, INNER])
        W["wv"] = split_pair("wv", [P, 2, INNER])
        W["wq"] = split_pair("wq", [P, KT, INNER])
        W["wo"] = split_pair("wo", [P, T0, D])
        W["qkv"] = split_pair("qkv", [P, KT, 3 * D])
        W["mid"] = split_pair("mid", [P, 2, 5 * D])
        W["up"] = split_pair("up", [P, KT, DM])
        W["down"] = split_pair("down", [P, TM, D])
        MIDCOL = {n: D * i for i, (n, _) in enumerate(MID)}

        ident = sb("ident", [P, P])
        identb = sb("identb", [P, P], BF16)
        causal = sb("causal", [P, P], BF16)
        blocks = sb("blocks", [P, 8])
        qmask = sb("qmask", [P, 2])
        qbias = sb("qbias", [P, 2, 2, T1])
        minus_half = sb("minus_half", [P, PAIR])
        prow = sb("prow", [40, P])
        pcol = sb("pcol", [P, 40])
        COL, at_col = {}, 0
        for name, ap, n in (
                ("g0", a["L0_xattn_gamma"], KT), ("b0", a["L0_xattn_beta"], KT),
                ("g1", a["L1_xattn_ln1_w"], KT), ("b1", a["L1_xattn_ln1_b"], KT),
                ("g2", a["L1_xattn_ln2_w"], KT), ("b2", a["L1_xattn_ln2_b"], KT),
                ("g3", a["L1_xattn_ln3_w"], KT), ("b3", a["L1_xattn_ln3_b"], KT),
                ("qkvb", a["L1_xattn_qkv_b"], 3 * T1), ("qb", a["L1_xattn_q_b"], T1), ("kb", a["L1_xattn_k_b"], T1),
                ("vb", a["L1_xattn_v_b"], T1), ("upb", a["L1_xattn_mlp1_b"], TM)):
            COL[name] = (at_col, n, ap)
            at_col += n
        assert at_col <= 40
        brow = sb("brow", [P, 4, D])
        BROWS = [a["L0_xattn_bo"], a["L1_xattn_proj_b"], a["L1_xattn_out_b"], a["L1_xattn_mlp2_b"]]

        def col(name, t):
            return pcol[:, COL[name][0] + t:COL[name][0] + t + 1]

        x_in = sb("x_in", [P, PAIR, D])
        c_in = sb("c_in", [P, PAIR, DC])
        m_in = sb("m_in", [P, 2, PAIR, T], U8)
        mask_add = sb("mask_add", [P, 2, PAIR, T], BF16)
        xres = sb("xres", [P, PAIR, D])
        xb = sb("xb", [P, PAIR, D])
        wait_pad = sb("wait_pad", [P, 1])
        stats = sb("stats", [P, PAIR, 6])
        mv = sb("mv", [P, PAIR, 2])
        vare = sb("vare", [P, PAIR])
        rstd = sb("rstd", [P, PAIR])
        xhat = sb("xhat", [P, PAIR, D])
        h_h, h_l = split_pair("h", [P, KT, TOK])
        c_h, c_l = split_pair("cT", [P, 2, TOK])
        probs = sb("probs", [P, 3, 4, T])
        pts = sb("pts", [P, 2, 4, T])
        nmax = sb("nmax", [P, 4, 4])
        rec = sb("rec", [P, 2, H])
        o_n = xhat
        h_f = probs[:, 0].rearrange("p (k b) t -> p k (b t)", k=KT)

        k2 = sb("k2", [P, T1, TOK])
        v2 = sb("v2", [P, PAIR, H, HD1 + 1])
        with ExitStack() as stack:
            stage = sb("stage", [P, 4, 2 * 1280], stack=stack)
        with ExitStack() as stack:
            q0 = sb("q0", [P, T0, TOK], stack=stack)
            k0 = sb("k0", [P, T0, TOK], stack=stack)
            v0 = sb("v0", [P, PAIR, H, HD0 + 1], stack=stack)
            oT_h = sb("oT_hi", [P, T0, TOK], F32R, stack)
            oT_l = sb("oT_lo", [P, T0, TOK], F32R, stack)
        with ExitStack() as stack:
            q1 = sb("q1", [P, 2, T1, TOK], stack=stack)
            k1 = sb("k1", [P, T1, TOK], stack=stack)
            v1 = sb("v1", [P, PAIR, H, HD1 + 1], stack=stack)
            g_f = sb("g_f", [P, 2, 2, TOK], stack=stack)
            g_h = sb("g_hi", [P, TM, TOK], F32R, stack)
            g_l = sb("g_lo", [P, TM, TOK], F32R, stack)
            o1T_h = sb("o1T_hi", [P, T1, TOK], F32R, stack)
            o1T_l = sb("o1T_lo", [P, T1, TOK], F32R, stack)

        sc = [ctx.enter_context(nc.psum_tensor(f"sc{n}", [P, 4, T], F32)) for n in range(3)]
        pt = [ctx.enter_context(nc.psum_tensor(f"pt{n}", [P, 4, T], F32)) for n in range(2)]
        mb = [ctx.enter_context(nc.psum_tensor(f"mb{n}", [P, 512], F32)) for n in range(3)]

        USES, USE = [], {}

        def use(stage_name, n, sem, k):
            USE[stage_name, n] = len(USES)
            USES.append((sem, k))

        use("xhatT", 0, "h_full", 2)
        use("cT", 0, "c_lo", 2)
        for n in range(4):
            use("k0", n, "k0_done", n + 1)
        for n in range(4):
            use("v0", n, "v0_done", n + 1)
        for n in range(4):
            use("q0", n, "q0_done", n + 1)
        for s in range(GROUPS + 1):
            if s < GROUPS:
                use("pv0", s, "on_ready", s + 1)
            if s >= 1:
                use("oT0", s - 1, "oT_lo", s)
        use("resid", 0, "resid_done", 1)
        use("k1", 0, "k1_done", 2)
        use("v1", 0, "v1_done", 1)
        use("xhatT", 1, "h_full", 4)
        use("q1", 0, "q1_done", 4)
        use("k1", 1, "k1_done", 4)
        use("v1", 1, "v1_done", 2)
        for b in range(PAIR):
            use("pv1", b, "on_ready", GROUPS + 1 + b)
        use("oT1", 0, "oT_lo", GROUPS + 2)
        use("resid", 1, "resid_done", 2)
        use("xhatT", 2, "h_full", 6)
        use("q1", 1, "q1_done", 8)
        for b in range(PAIR):
            use("pv2", b, "on_ready", GROUPS + 3 + b)
        use("oT2", 0, "oT_lo", GROUPS + 4)
        use("resid", 2, "resid_done", 3)
        use("xhatT", 3, "h_full", 8)
        for n in range(4):
            use("up", n, "gelu_done", 2 * n + 2)
        use("resid", 3, "resid_done", 4)
        use("resid", 4, "resid_done", 5)
        assert len(USES) % 3 == 0

        def bank(stage_name, n=0):
            return mb[USE[stage_name, n] % 3]

        def head0(g, j):
            gg, par = (g % 4) // 2, g % 2
            return 8 * gg + 2 * j + par

        def head1(g, j):
            return 8 * (j // 2) + 2 * (g % 4) + j % 2

        x_v = a["x"].rearrange("(i b) t d -> i t b d", b=PAIR)
        c_v = a["ctx_768"].rearrange("(i b) t d -> i t b d", b=PAIR)
        y_v = out.rearrange("(i b) t d -> i b t d", b=PAIR)
        m_v = [a[n].rearrange("(i b) t -> i b t", b=PAIR) for n in ("mask_BxS_bf0", "mask_BxS2_bf0")]

        def raw(name):
            slot = stage[:, [n for n, _ in WEIGHTS].index(name) % 4, :]
            if name in ("wk", "wv"):
                v = slot[:, 0:2 * INNER].rearrange("p (k n) -> p k n", k=2)
                w = dict(WEIGHTS)[name]
                return v, [(v[:, 0, :], w[0:P, :]), (v[0:DC1, 1, :], w[P:DC, :])]
            if name == "wo":
                v = slot[:, 0:T0 * D].rearrange("p (t n) -> p t n", t=T0)
                w = dict(WEIGHTS)[name].rearrange("(g j l r d) n -> g r l d j n", g=2, j=2, l=2, r=2)
                return v, [(v[HD0 * l:HD0 * l + HD0, 4 * g + 2 * r:4 * g + 2 * r + 2, :], w[g, r, l])
                           for g in range(2) for r in range(2) for l in range(2)]
            if name == "mid":
                v = slot.rearrange("p (k n) -> p k n", k=2)
                loads = []
                for n, full in MID:
                    c0 = MIDCOL[n]
                    w = a[full]
                    loads.append((v[:, 0, c0:c0 + D], w[0:P, :]))
                    rows = w.shape[0] - P
                    loads.append((v[0:rows, 1, c0:c0 + D], w[P:P + rows, :]))
                return v, loads
            w = dict(WEIGHTS)[name]
            k = w.shape[0] // P
            v = slot[:, 0:k * w.shape[1]].rearrange("p (k n) -> p k n", k=k)
            return v, [(v, w.rearrange("(k p) n -> p k n", p=P))]

        def pieces(name):
            if name in ("wk", "wv"):
                return [(P, slice(0, 1), slice(0, INNER)), (DC1, slice(1, 2), slice(0, INNER))]
            if name == "mid":
                return [(P, slice(0, 1), slice(0, 5 * D)), (DC1, slice(1, 2), slice(0, 2 * D)),
                        (P, slice(1, 2), slice(2 * D, 5 * D))]
            n = W[name][0].shape
            return [(P, slice(0, n[1]), slice(0, n[2]))]

        NPIECE = [0]
        for n, _ in WEIGHTS:
            NPIECE.append(NPIECE[-1] + len(pieces(n)))

        block = ctx.enter_context(nc.Block())

        @block.sync
        def _(sp):
            def load_turn(i):
                sp.dma_start(x_in[:], x_v[i]).then_inc(S["x_loaded"], 16)
                sp.dma_start(c_in[:], c_v[i]).then_inc(S["c_loaded"], 16)
                for m in range(2):
                    for b in range(PAIR):
                        sp.dma_start(m_in[:, m, b, :], m_v[m][i, b:b + 1, :].to_broadcast([P, T])) \
                          .then_inc(S["masks_loaded"], 16)

            def store_turn(i):
                for b in range(PAIR):
                    sp.wait_ge(S["resid_done"], at("resid_done", i, 4 + b))
                    sp.dma_start(y_v[i, b], xres[:, b, :]).then_inc(S["y_stored"], 16)

            load_turn(0)
            for n, (name, _) in enumerate(WEIGHTS):
                if n >= 4:
                    sp.wait_ge(S["w_lo_done"], NPIECE[n - 3])
                for dst, src in raw(name)[1]:
                    sp.dma_start(dst, src).then_inc(w_loaded[n], 16)
            with sp.Fori(1, TURNS) as i:
                sp.wait_ge(S["xhat_ready"], at("xhat_ready", i - 1, 2))
                sp.wait_ge(S["xb_ready"], at("xb_ready", i - 1, 1))
                sp.wait_ge(S["cT_ready"], at("cT_ready", i - 1, 1))
                sp.wait_ge(S["masks_ready"], at("masks_ready", i - 1, 2))
                load_turn(i)
                store_turn(i - 1)
            store_turn(TURNS - 1)
            sp.wait_ge(S["y_stored"], at("y_stored", TURNS, 0))

        @block.gpsimd
        def _(pool):
            nc.gpsimd.memset(ident[:], 0.0).then_inc(S["consts_built"], 1)
            nc.gpsimd.memset(causal[:], 0.0).then_inc(S["consts_built"], 1)
            nc.gpsimd.memset(blocks[:], 1.0).then_inc(S["consts_built"], 1)
            nc.gpsimd.memset(minus_half[:], -0.5).then_inc(S["consts_built"], 1)
            pool.wait_ge(S["consts_built"], 4)
            nc.gpsimd.affine_select(out=ident[:], in_=ident[:], compare_op=ALU.not_equal, fill=1.0, base=0,
                                    pattern=[[-1, P]], channel_multiplier=1).then_inc(S["consts_built"], 1)
            nc.gpsimd.affine_select(out=causal[:], in_=causal[:], compare_op=ALU.is_ge, fill=MASKED, base=0,
                                    pattern=[[-1, P]], channel_multiplier=1).then_inc(S["consts_built"], 1)
            nc.gpsimd.affine_select(out=blocks[:], in_=blocks[:], compare_op=ALU.is_ge, fill=0.0, base=0,
                                    pattern=[[-HD1, 8]], channel_multiplier=1).then_inc(S["consts_built"], 1)
            pool.wait_ge(S["consts_built"], 7)
            nc.gpsimd.affine_select(out=blocks[:], in_=blocks[:], compare_op=ALU.is_ge, fill=0.0, base=HD1 - 1,
                                    pattern=[[HD1, 8]], channel_multiplier=-1).then_inc(S["consts_built"], 1)
            for name, (c0, n, ap) in COL.items():
                pool.dma_start(prow[c0:c0 + n, :], ap.rearrange("(t p) -> t p", p=P)).then_inc(S["params_loaded"], 16)
            for n, ap in enumerate(BROWS):
                pool.dma_start(brow[:, n, :], ap.rearrange("(o d) -> o d", o=1).to_broadcast([P, D])) \
                    .then_inc(S["params_loaded"], 16)
            pool.wait_ge(S["params_loaded"], 16 * (len(COL) + len(BROWS)))

            def norm_scale(i, n):
                pool.wait_ge(S["ln_var"], at("ln_var", i, n + 1))
                nc.gpsimd.tensor_tensor(rstd[:], vare[:], minus_half[:], ALU.pow).then_inc(S["ln_rstd"], 1)

            def add_bias(i, n):
                src = x_in if n == 0 else xres
                if n == 0:
                    pool.wait_ge(S["x_loaded"], at("x_loaded", i, 16))
                    pool.wait_ge(S["resid_done"], at("resid_done", i, 0))
                else:
                    pool.wait_ge(S["resid_done"], at("resid_done", i, n))
                nc.gpsimd.tensor_tensor(xb[:], src[:], brow[:, n:n + 1, :].to_broadcast([P, PAIR, D]), ALU.add) \
                    .then_inc(S["xb_ready"], 1)

            with pool.Fori(0, TURNS) as i:
                norm_scale(i, 0)
                add_bias(i, 0)
                for n in range(1, 4):
                    norm_scale(i, n)
                    add_bias(i, n)

        @block.scalar
        def _(act):
            for n, (name, _) in enumerate(WEIGHTS):
                v, loads = raw(name)
                act.wait_ge(w_loaded[n], 16 * len(loads))
                for rows, k, c in pieces(name):
                    nc.scalar.activation(W[name][0][0:rows, k, c], v[0:rows, k, c], ACT.Copy) \
                        .then_inc(S["w_hi_done"], 1)
            act.wait_ge(S["prepared"], 1)
            act.wait_ge(S["w_lo_done"], NPIECE[-1])

            def h_high(i, n):
                act.wait_ge(S["h_full"], at("h_full", i, 2 * n + 2))
                nc.scalar.activation(h_h[:], h_f[:], ACT.Copy).then_inc(S["h_hi"], 1)

            def groups(i, att, lead):
                base = att * GROUPS
                for s in range(GROUPS + LAG_O):
                    g = s
                    if g < GROUPS:
                        act.wait_ge(S["nmax_ready"], at("nmax_ready", i, base + g + 1))
                        for j in range(4):
                            e = nc.scalar.activation(probs[:, g % 3, j, :], sc[g % 3 if not att else (base + g) % 3][:, j, :],
                                                     ACT.Exp, bias=nmax[:, (base + g) % 4, j:j + 1])
                        e.then_inc(S["exp_done"], 1)
                    g = s - LAG_T
                    if 0 <= g < GROUPS:
                        act.wait_ge(S["pt_ready"], at("pt_ready", i, base + g + 1))
                        if g >= 2:
                            act.wait_ge(S["pv_done"], at("pv_done", i, base + g - 1))
                        nc.scalar.activation(pts[:, g % 2], pt[g % 2][:], ACT.Copy).then_inc(S["pts_ready"], 1)
                    g = s - LAG_O
                    if lead and 0 <= g < GROUPS:
                        act.wait_ge(S["oT_ready"], at("oT_ready", i, g + 1))
                        b, t = g // 4, 2 * (g % 4)
                        nc.scalar.activation(oT_h[:, t:t + 2, b * T:(b + 1) * T],
                                             bank("oT0", g)[:, 0:2 * T].rearrange("p (t c) -> p t c", t=2), ACT.Copy) \
                            .then_inc(S["oT_hi"], 1)

            def outT_high(i, att, vbias):
                act.wait_ge(S["oT_ready"], at("oT_ready", i, GROUPS + att))
                for t in range(T1):
                    nc.scalar.activation(o1T_h[:, t, :], bank(f"oT{att}")[:, t * TOK:(t + 1) * TOK], ACT.Identity,
                                         bias=vbias(t)).then_inc(S["oT_hi"], 1)

            def queries(i, att):
                act.wait_ge(S["q1_ready"], at("q1_ready", i, att + 1))
                for par in range(2):
                    for t in range(T1):
                        nc.scalar.activation(q1[:, par, t, :], bank("q1", att)[:, t * TOK:(t + 1) * TOK], ACT.Identity,
                                             scale=qmask[:, par:par + 1], bias=qbias[:, att, par, t:t + 1]) \
                            .then_inc(S["q1_done"], 1)

            with act.Fori(0, TURNS) as i:
                h_high(i, 0)
                act.wait_ge(S["cT_ready"], at("cT_ready", i, 1))
                for k in range(2):
                    nc.scalar.activation(c_h[0:CK[k], k, :], bank("cT")[0:CK[k], k * TOK:(k + 1) * TOK], ACT.Copy) \
                        .then_inc(S["c_hi"], 1)
                for n in range(4):
                    act.wait_ge(S["k0_ready"], at("k0_ready", i, n + 1))
                    nc.scalar.activation(k0[:, 2 * n:2 * n + 2, :].rearrange("p t c -> p (t c)"), bank("k0", n)[:],
                                         ACT.Copy).then_inc(S["k0_done"], 1)
                for n in range(4):
                    act.wait_ge(S["q0_ready"], at("q0_ready", i, n + 1))
                    nc.scalar.activation(q0[:, 2 * n:2 * n + 2, :].rearrange("p t c -> p (t c)"), bank("q0", n)[:],
                                         ACT.Copy).then_inc(S["q0_done"], 1)
                groups(i, 0, True)
                act.wait_ge(S["k1_ready"], at("k1_ready", i, 1))
                for t in range(T1):
                    nc.scalar.activation(k2[:, t, :], bank("k1", 0)[:, t * TOK:(t + 1) * TOK], ACT.Identity,
                                         bias=col("kb", t)).then_inc(S["k1_done"], 1)
                h_high(i, 1)
                queries(i, 0)
                act.wait_ge(S["k1_ready"], at("k1_ready", i, 2))
                for t in range(T1):
                    nc.scalar.activation(k1[:, t, :], bank("k1", 1)[:, t * TOK:(t + 1) * TOK], ACT.Identity,
                                         bias=col("qkvb", T1 + t)).then_inc(S["k1_done"], 1)
                groups(i, 1, False)
                outT_high(i, 1, lambda t: col("qkvb", 2 * T1 + t))
                h_high(i, 2)
                queries(i, 1)
                groups(i, 2, False)
                outT_high(i, 2, lambda t: col("vb", t))
                h_high(i, 3)
                for n in range(4):
                    act.wait_ge(S["up_ready"], at("up_ready", i, n + 1))
                    if n >= 2:
                        act.wait_ge(S["g_lo"], at("g_lo", i, n - 1))
                    for t in range(2):
                        nc.scalar.activation(g_f[:, n % 2, t, :], bank("up", n)[:, t * TOK:(t + 1) * TOK], ACT.Gelu,
                                             bias=col("upb", 2 * n + t)).then_inc(S["gelu_done"], 1)

        @block.vector
        def _(dve):
            for n, (name, _) in enumerate(WEIGHTS):
                v, loads = raw(name)
                for m, (rows, k, c) in enumerate(pieces(name)):
                    dve.wait_ge(S["w_hi_done"], NPIECE[n] + m + 1)
                    dve.wait_ge(w_loaded[n], 16 * len(loads))
                    nc.vector.tensor_tensor(W[name][1][0:rows, k, c], v[0:rows, k, c], W[name][0][0:rows, k, c],
                                            ALU.subtract).then_inc(S["w_lo_done"], 1)
            dve.wait_ge(S["consts_built"], 8)
            nc.vector.tensor_copy(identb[:], ident[:]).then_inc(S["prep_steps"], 1)
            nc.vector.tensor_reduce(qmask[:], blocks[:].rearrange("p (a r) -> p r a", r=2), AX, ALU.add) \
                .then_inc(S["prep_steps"], 1)
            dve.wait_ge(S["prep_steps"], 2)
            nc.vector.tensor_scalar(qmask[:], qmask[:], float(HD1) ** -0.5, None, ALU.mult).then_inc(S["prep_steps"], 1)
            dve.wait_ge(S["prep_steps"], 3)
            dve.wait_ge(S["params_turned"], 1)
            nc.vector.tensor_copy(pcol[:, 0:at_col], sc[0][:, 0, 0:at_col]).then_inc(S["prep_steps"], 1)
            dve.wait_ge(S["prep_steps"], 4)
            for att, name in enumerate(("qkvb", "qb")):
                for par in range(2):
                    nc.vector.tensor_scalar(qbias[:, att, par, :], pcol[:, COL[name][0]:COL[name][0] + T1],
                                            qmask[:, par:par + 1], None, ALU.mult).then_inc(S["prep_steps"], 1)
            nc.vector.memset(v2[:, :, :, HD1:HD1 + 1], 1.0).then_inc(S["ones_set"], 1)
            dve.wait_ge(S["prep_steps"], 8)
            nc.vector.memset(wait_pad[:], 0.0).then_inc(S["resid_done"], CREDIT["resid_done"])
            nc.vector.memset(nmax[:], 0.0).then_inc(S["y_stored"], CREDIT["y_stored"])
            dve.wait_ge(S["resid_done"], 1)
            dve.wait_ge(S["y_stored"], 1)
            nc.vector.memset(o_n[:], 0.0).then_inc(S["prepared"], 1)
            dve.wait_ge(S["prepared"], 1)

            def norm(i, n):
                src = x_in if n == 0 else xres
                if n == 0:
                    dve.wait_ge(S["x_loaded"], at("x_loaded", i, 16))
                else:
                    dve.wait_ge(S["resid_done"], at("resid_done", i, n))
                for b in range(PAIR):
                    nc.vector.bn_stats(stats[:, b, :], src[:, b, :]).then_inc(S["ln_stats"], 1)
                dve.wait_ge(S["ln_stats"], at("ln_stats", i, 3 * n + 2))
                nc.vector.memset(wait_pad[:], 0.0).then_inc(S["ln_stats"], 1)
                for b in range(PAIR):
                    nc.vector.bn_aggr(mv[:, b, :], stats[:, b, :]).then_inc(S["ln_aggr"], 1)
                dve.wait_ge(S["ln_aggr"], at("ln_aggr", i, 2 * n + 2))
                nc.vector.tensor_scalar(vare[:], mv[:, :, 1], EPS, None, ALU.add).then_inc(S["ln_var"], 1)
                dve.wait_ge(S["ln_rstd"], at("ln_rstd", i, n + 1))
                for b in range(PAIR):
                    nc.vector.tensor_scalar(xhat[:, b, :], src[:, b, :], mv[:, b, 0:1], rstd[:, b:b + 1],
                                            ALU.subtract, ALU.mult).then_inc(S["xhat_ready"], 1)

            def scale_shift(i, n):
                dve.wait_ge(S["xhatT_ready"], at("xhatT_ready", i, n + 1))
                for k in range(KT):
                    nc.vector.tensor_scalar(h_f[:, k, :], bank("xhatT", n)[:, k * TOK:(k + 1) * TOK], col(f"g{n}", k),
                                            col(f"b{n}", k), ALU.mult, ALU.add).then_inc(S["h_full"], 1)

            def h_low(i, n):
                dve.wait_ge(S["h_hi"], at("h_hi", i, n + 1))
                dve.wait_ge(S["h_full"], at("h_full", i, 2 * n + 2))
                nc.vector.tensor_tensor(h_l[:], h_f[:], h_h[:], ALU.subtract).then_inc(S["h_lo"], 1)

            def row_max(i, att, g):
                n = att * GROUPS + g
                dve.wait_ge(S["scores_ready"], at("scores_ready", i, n + 1))
                m = nmax[:, n % 4, :]
                r = nc.vector.tensor_reduce(m, sc[n % 3][:], AX, ALU.max, negate=True)
                if att == 0:
                    r.then_inc(S["nmax_ready"], 1)
                    return
                r.then_inc(S["raw_max"], 1)
                dve.wait_ge(S["raw_max"], at("raw_max", i, n - GROUPS + 1))
                nc.vector.tensor_scalar(m, m, 4.0, 0.25, ALU.mult, ALU.mult).then_inc(S["nmax_ready"], 1)

            def residual(i, n):
                dve.wait_ge(S["resid_ready"], at("resid_ready", i, n + 1))
                dve.wait_ge(S["xb_ready"], at("xb_ready", i, min(n, 3) + 1))
                if n == 0:
                    dve.wait_ge(S["y_stored"], at("y_stored", i, 0))
                if n < 3:
                    nc.vector.tensor_tensor(xres[:].rearrange("p b d -> p (b d)"), bank("resid", n)[:],
                                            xb[:].rearrange("p b d -> p (b d)"), ALU.add).then_inc(S["resid_done"], 1)
                else:
                    nc.vector.tensor_tensor(xres[:, n - 3, :], bank("resid", n)[:, 0:D], xb[:, n - 3, :], ALU.add) \
                        .then_inc(S["resid_done"], 1)

            def values(i, n, dst):
                dve.wait_ge(S["v1_ready"], at("v1_ready", i, n + 1))
                nc.vector.tensor_copy(dst[:, :, :, 0:HD1],
                                      bank("v1", n)[:].rearrange("p (b h d) -> p b h d", b=PAIR, h=H)) \
                    .then_inc(S["v1_done"], 1)

            def groups1(i, att):
                for s in range(GROUPS + LAG_PV):
                    if s < GROUPS:
                        row_max(i, att, s)
                    g = s - LAG_PV
                    if g >= 0 and g % 4 == 3:
                        b = g // 4
                        dve.wait_ge(S["pv_done"], at("pv_done", i, att * GROUPS + g + 1))
                        o = bank(f"pv{att}", b)[:, 0:H * (HD1 + 1)].rearrange("p (h d) -> p h d", h=H)
                        nc.vector.reciprocal(rec[:, b, :], o[:, :, HD1]).then_inc(S["recip1"], 1)
                        dve.wait_ge(S["recip1"], at("recip1", i, 2 * (att - 1) + b + 1))
                        nc.vector.tensor_tensor(o_n[:, b, :].rearrange("p (h d) -> p h d", h=H), o[:, :, 0:HD1],
                                                rec[:, b, :].unsqueeze(2).to_broadcast([P, H, HD1]), ALU.mult) \
                            .then_inc(S["on_ready"], 1)

            def outT_low(i, att, vbias):
                dve.wait_ge(S["oT_hi"], at("oT_hi", i, GROUPS + 2 * att))
                for t in range(T1):
                    nc.vector.scalar_tensor_tensor(out=o1T_l[:, t, :], in0=bank(f"oT{att}")[:, t * TOK:(t + 1) * TOK],
                                                   scalar=vbias(t), in1=o1T_h[:, t, :], op0=ALU.add,
                                                   op1=ALU.subtract).then_inc(S["oT_lo"], 1)

            with dve.Fori(0, TURNS) as i:
                norm(i, 0)
                scale_shift(i, 0)
                dve.wait_ge(S["masks_loaded"], at("masks_loaded", i, 64))
                nc.vector.scalar_tensor_tensor(out=mask_add[:, 0], in0=m_in[:, 0], scalar=MASKED,
                                               in1=causal[:, None, :].to_broadcast([P, PAIR, T]), op0=ALU.mult,
                                               op1=ALU.min).then_inc(S["masks_ready"], 1)
                nc.vector.tensor_scalar(mask_add[:, 1], m_in[:, 1], MASKED, None, ALU.mult) \
                    .then_inc(S["masks_ready"], 1)
                h_low(i, 0)
                dve.wait_ge(S["c_hi"], at("c_hi", i, 2))
                for k in range(2):
                    nc.vector.tensor_tensor(c_l[0:CK[k], k, :], bank("cT")[0:CK[k], k * TOK:(k + 1) * TOK],
                                            c_h[0:CK[k], k, :], ALU.subtract).then_inc(S["c_lo"], 1)
                nc.vector.memset(v0[:, :, :, HD0:HD0 + 1], 1.0)
                for n in range(4):
                    dve.wait_ge(S["v0_ready"], at("v0_ready", i, n + 1))
                    nc.vector.tensor_copy(v0[:, n // 2, 8 * (n % 2):8 * (n % 2) + 8, 0:HD0],
                                          bank("v0", n)[:].rearrange("p (h d) -> p h d", h=8)).then_inc(S["v0_done"], 1)
                for s in range(GROUPS + LAG_O):
                    if s < GROUPS:
                        row_max(i, 0, s)
                    g = s - LAG_PV
                    if 0 <= g < GROUPS:
                        dve.wait_ge(S["pv_done"], at("pv_done", i, g + 1))
                        o = bank("pv0", g)[:, 0:4 * (HD0 + 1)].rearrange("p (h d) -> p h d", h=4)
                        r = rec[:, g % 2, 0:4]
                        nc.vector.reciprocal(r, o[:, :, HD0]).then_inc(S["recip0"], 1)
                        dve.wait_ge(S["recip0"], at("recip0", i, g + 1))
                        nc.vector.scalar_tensor_tensor(out=o_n[:, g % 2, :].rearrange("p (h d) -> p h d", h=4),
                                                       in0=o[:, :, 0:HD0], scalar=float(HD0) ** -0.5,
                                                       in1=r.unsqueeze(2).to_broadcast([P, 4, HD0]),
                                                       op0=ALU.mult, op1=ALU.mult).then_inc(S["on_ready"], 1)
                    g = s - LAG_O
                    if g >= 0:
                        dve.wait_ge(S["oT_hi"], at("oT_hi", i, g + 1))
                        b, t = g // 4, 2 * (g % 4)
                        nc.vector.tensor_tensor(oT_l[:, t:t + 2, b * T:(b + 1) * T],
                                                bank("oT0", g)[:, 0:2 * T].rearrange("p (t c) -> p t c", t=2),
                                                oT_h[:, t:t + 2, b * T:(b + 1) * T], ALU.subtract).then_inc(S["oT_lo"], 1)
                residual(i, 0)
                values(i, 0, v2)
                norm(i, 1)
                scale_shift(i, 1)
                h_low(i, 1)
                nc.vector.memset(v1[:, :, :, HD1:HD1 + 1], 1.0)
                values(i, 1, v1)
                groups1(i, 1)
                outT_low(i, 1, lambda t: col("qkvb", 2 * T1 + t))
                residual(i, 1)
                norm(i, 2)
                scale_shift(i, 2)
                h_low(i, 2)
                groups1(i, 2)
                outT_low(i, 2, lambda t: col("vb", t))
                residual(i, 2)
                norm(i, 3)
                scale_shift(i, 3)
                h_low(i, 3)
                for n in range(4):
                    dve.wait_ge(S["gelu_done"], at("gelu_done", i, 2 * n + 2))
                    nc.vector.tensor_copy(g_h[:, 2 * n:2 * n + 2, :], g_f[:, n % 2]).then_inc(S["g_hi"], 1)
                    dve.wait_ge(S["g_hi"], at("g_hi", i, n + 1))
                    nc.vector.tensor_tensor(g_l[:, 2 * n:2 * n + 2, :], g_f[:, n % 2], g_h[:, 2 * n:2 * n + 2, :],
                                            ALU.subtract).then_inc(S["g_lo"], 1)
                residual(i, 3)
                residual(i, 4)

        @block.tensor
        def _(pe):
            pe.wait_ge(S["consts_built"], 8)
            pe.wait_ge(S["params_loaded"], 16 * (len(COL) + len(BROWS)))
            nc.tensor.transpose(sc[0][:, 0, 0:at_col], prow[0:at_col, :], ident[0:at_col, 0:at_col]) \
                .then_inc(S["params_turned"], 1)
            pe.wait_ge(S["w_lo_done"], NPIECE[-1])
            pe.wait_ge(S["prepared"], 1)

            def free(i, stage_name, n=0):
                u = USE[stage_name, n]
                if u >= 3:
                    sem, k = USES[u - 3]
                    pe.wait_ge(S[sem], at(sem, i, k))

            def product(dst, lhs, rhs):
                n = len(lhs)
                for k in range(n):
                    for p, (l, r) in enumerate(((0, 0), (0, 1), (1, 0))):
                        m = nc.tensor.matmul(dst, lhs[k][l], rhs[k][r], start=(k == 0 and p == 0),
                                             stop=(k == n - 1 and p == 2))
                return m

            def w_tiles(name, rows, c0, cols):
                return [(W[name][0][0:r, k, c0:c0 + cols], W[name][1][0:r, k, c0:c0 + cols])
                        for k, r in enumerate(rows)]

            def a_tiles(pair, rows, c0, cols):
                return [(pair[0][0:r, k, c0:c0 + cols], pair[1][0:r, k, c0:c0 + cols]) for k, r in enumerate(rows)]

            FULL = [P] * KT

            def feature_major(i, stage_name, n, sem, name, c0, src, rows, tiles=2):
                free(i, stage_name, n)
                for t in range(tiles):
                    m = product(bank(stage_name, n)[:, t * TOK:(t + 1) * TOK],
                                w_tiles(name, rows, c0 + t * P, P), a_tiles(src, rows, 0, TOK))
                m.then_inc(S[sem], 1)

            def token_major(i, stage_name, n, sem, name, c0, src, rows, seqs=range(PAIR)):
                free(i, stage_name, n)
                for q, b in enumerate(seqs):
                    m = product(bank(stage_name, n)[:, q * D:(q + 1) * D],
                                a_tiles(src, rows, b * T, T), w_tiles(name, rows, c0, D))
                m.then_inc(S[sem], 1)

            def transpose_norm(i, n):
                free(i, "xhatT", n)
                pe.wait_ge(S["xhat_ready"], at("xhat_ready", i, 2 * n + 2))
                for b in range(PAIR):
                    for k in range(KT):
                        m = nc.tensor.transpose(bank("xhatT", n)[:, k * TOK + b * T:k * TOK + (b + 1) * T],
                                                xhat[:, b, k * P:(k + 1) * P], ident[:])
                m.then_inc(S["xhatT_ready"], 1)

            def score(i, att, g):
                n = att * GROUPS + g
                b = g // 4
                dst = sc[n % 3]
                tok = slice(b * T, (b + 1) * T)
                if att == 0:
                    for j in range(4):
                        h = head0(g, j)
                        r = slice(HD0 * (h % 2), HD0 * (h % 2) + HD0)
                        m = nc.tensor.matmul(dst[:, j, :], q0[r, h // 2, tok], k0[r, h // 2, tok], start=True, stop=True)
                else:
                    keys = k1 if att == 1 else k2
                    nc.tensor.matmul(dst[:], identb[:], mask_add[:, att - 1, b:b + 1, :].to_broadcast([P, 4, T]),
                                     start=True, stop=False)
                    r = slice(32 * (g % 4), 32 * (g % 4) + 32)
                    for j in range(4):
                        m = nc.tensor.matmul(dst[:, j, :], q1[r, j % 2, j // 2, tok], keys[r, j // 2, tok],
                                             start=False, stop=(j == 3))
                m.then_inc(S["scores_ready"], 1)

            def turn_probs(i, att, g):
                n = att * GROUPS + g
                pe.wait_ge(S["exp_done"], at("exp_done", i, n + 1))
                for j in range(4):
                    m = nc.tensor.transpose(pt[g % 2][:, j, :], probs[:, g % 3, j, :], ident[:])
                m.then_inc(S["pt_ready"], 1)

            def weigh(i, att, g):
                n, b = att * GROUPS + g, g // 4
                if att == 0:
                    free(i, "pv0", g)
                elif g % 4 == 0:
                    free(i, f"pv{att}", b)
                pe.wait_ge(S["pts_ready"], at("pts_ready", i, n + 1))
                for j in range(4):
                    if att == 0:
                        dst = bank("pv0", g)[:, j * (HD0 + 1):(j + 1) * (HD0 + 1)]
                        v = v0[:, b, head0(g, j), :]
                    else:
                        h = head1(g, j)
                        dst = bank(f"pv{att}", b)[:, h * (HD1 + 1):(h + 1) * (HD1 + 1)]
                        v = (v1 if att == 1 else v2)[:, b, h, :]
                    m = nc.tensor.matmul(dst, pts[:, g % 2, j, :], v, start=True, stop=True)
                m.then_inc(S["pv_done"], 1)

            def turn_out0(i, g):
                free(i, "oT0", g)
                pe.wait_ge(S["on_ready"], at("on_ready", i, g + 1))
                for k in range(2):
                    m = nc.tensor.transpose(bank("oT0", g)[:, k * P:(k + 1) * P], o_n[:, g % 2, k * P:(k + 1) * P],
                                            ident[:])
                m.then_inc(S["oT_ready"], 1)

            def turn_out1(i, att):
                free(i, f"oT{att}")
                pe.wait_ge(S["on_ready"], at("on_ready", i, GROUPS + 2 * att))
                for b in range(PAIR):
                    for k in range(T1):
                        m = nc.tensor.transpose(bank(f"oT{att}")[:, k * TOK + b * T:k * TOK + (b + 1) * T],
                                                o_n[:, b, k * P:(k + 1) * P], ident[:])
                m.then_inc(S["oT_ready"], 1)

            def attention(i, att):
                for s in range(GROUPS + (LAG_O if att == 0 else LAG_PV)):
                    if s < GROUPS:
                        score(i, att, s)
                    if 0 <= s - LAG_T < GROUPS:
                        turn_probs(i, att, s - LAG_T)
                    if 0 <= s - LAG_PV < GROUPS:
                        weigh(i, att, s - LAG_PV)
                    if att == 0 and s >= LAG_O:
                        turn_out0(i, s - LAG_O)

            with pe.Fori(0, TURNS) as i:
                pe.wait_ge(S["resid_done"], at("resid_done", i, 0))
                transpose_norm(i, 0)
                pe.wait_ge(S["c_loaded"], at("c_loaded", i, 16))
                for b in range(PAIR):
                    for k in range(2):
                        m = nc.tensor.transpose(bank("cT")[0:CK[k], k * TOK + b * T:k * TOK + (b + 1) * T],
                                                c_in[:, b, k * P:k * P + CK[k]], ident[:])
                m.then_inc(S["cT_ready"], 1)
                pe.wait_ge(S["c_lo"], at("c_lo", i, 2))
                for n in range(4):
                    feature_major(i, "k0", n, "k0_ready", "wk", 2 * P * n, (c_h, c_l), CK)
                for n in range(4):
                    free(i, "v0", n)
                    product(bank("v0", n)[:], a_tiles((c_h, c_l), CK, (n // 2) * T, T),
                            w_tiles("wv", CK, 512 * (n % 2), 512)).then_inc(S["v0_ready"], 1)
                pe.wait_ge(S["h_lo"], at("h_lo", i, 1))
                for n in range(4):
                    feature_major(i, "q0", n, "q0_ready", "wq", 2 * P * n, (h_h, h_l), FULL)
                pe.wait_ge(S["q0_done"], at("q0_done", i, 4))
                pe.wait_ge(S["v0_done"], at("v0_done", i, 4))
                attention(i, 0)
                pe.wait_ge(S["oT_lo"], at("oT_lo", i, GROUPS))
                token_major(i, "resid", 0, "resid_ready", "wo", 0, (oT_h, oT_l), [P] * T0)
                feature_major(i, "k1", 0, "k1_ready", "mid", MIDCOL["k2"], (c_h, c_l), CK)
                token_major(i, "v1", 0, "v1_ready", "mid", MIDCOL["v2"], (c_h, c_l), CK)
                transpose_norm(i, 1)
                pe.wait_ge(S["h_lo"], at("h_lo", i, 2))
                feature_major(i, "q1", 0, "q1_ready", "qkv", 0, (h_h, h_l), FULL)
                feature_major(i, "k1", 1, "k1_ready", "qkv", D, (h_h, h_l), FULL)
                token_major(i, "v1", 1, "v1_ready", "qkv", 2 * D, (h_h, h_l), FULL)
                pe.wait_ge(S["masks_ready"], at("masks_ready", i, 2))
                pe.wait_ge(S["k1_done"], at("k1_done", i, 4))
                pe.wait_ge(S["v1_done"], at("v1_done", i, 2))
                attention(i, 1)
                turn_out1(i, 1)
                pe.wait_ge(S["oT_lo"], at("oT_lo", i, GROUPS + 2))
                token_major(i, "resid", 1, "resid_ready", "mid", MIDCOL["pr"], (o1T_h, o1T_l), FULL)
                transpose_norm(i, 2)
                pe.wait_ge(S["h_lo"], at("h_lo", i, 3))
                feature_major(i, "q1", 1, "q1_ready", "mid", MIDCOL["q2"], (h_h, h_l), FULL)
                pe.wait_ge(S["q1_done"], at("q1_done", i, 8))
                attention(i, 2)
                turn_out1(i, 2)
                pe.wait_ge(S["oT_lo"], at("oT_lo", i, GROUPS + 4))
                token_major(i, "resid", 2, "resid_ready", "mid", MIDCOL["ou"], (o1T_h, o1T_l), FULL)
                transpose_norm(i, 3)
                pe.wait_ge(S["h_lo"], at("h_lo", i, 4))
                for n in range(4):
                    feature_major(i, "up", n, "up_ready", "up", 2 * P * n, (h_h, h_l), FULL)
                pe.wait_ge(S["g_lo"], at("g_lo", i, 4))
                for b in range(PAIR):
                    token_major(i, "resid", 3 + b, "resid_ready", "down", 0, (g_h, g_l), [P] * TM, seqs=[b])


_OUT = ((32, 128, 256), 'float32')


def kernel(**inputs):
    import numpy as _np
    import concourse.bacc as _bacc
    from concourse import mybir as _mybir
    from concourse.bass_utils import run_bass_kernel_spmd as _run

    nc = _bacc.Bacc("TRN2", target_bir_lowering=False, num_devices=1)
    arrays, args = {}, {}
    for name, value in inputs.items():
        x = _np.ascontiguousarray(value)
        arrays[f"in_{name}_dram"] = x
        args[name] = nc.dram_tensor(f"in_{name}_dram", x.shape, _mybir.dt.from_np(x.dtype), kind="ExternalInput").ap()
    out = nc.dram_tensor("out_0_dram", _OUT[0], _mybir.dt.float32, kind="ExternalOutput").ap()
    decoder_kernel(nc, args, out)
    r = _run(nc, [arrays], core_ids=[0])
    return r.results[0]["out_0_dram"]
```

```python
from contextlib import ExitStack

import concourse.bass as bass
from concourse import mybir

F32 = mybir.dt.float32
F32R = mybir.dt.float32r
BF16 = mybir.dt.bfloat16
U8 = mybir.dt.uint8
ALU = mybir.AluOpType
ACT = mybir.ActivationFunctionType
AX = mybir.AxisListType.X

P = 128
PAIR = 2
EPS = 1e-5
MASKED = -3.0e38
LAG_T, LAG_PV, LAG_O = 2, 3, 4

PER = dict(
    x_loaded=16, c_loaded=16, masks_loaded=64, y_stored=32,
    ln_stats=16, ln_aggr=8, ln_var=8, ln_rstd=8, xhat_ready=8, xhatT_ready=8, h_full=8, h_hi=8, h_lo=8,
    cT_ready=1, c_hi=2, c_lo=2, masks_ready=2,
    k0_ready=4, k0_done=4, v0_ready=4, v0_done=4, q0_ready=4, q0_done=4,
    scores_ready=24, raw_max=16, nmax_ready=24, exp_done=24, pt_ready=24, pts_ready=24, pv_done=24,
    recip0=8, on_ready=12, recip1=4, oT_ready=12, oT_hi=12, oT_lo=12,
    resid_ready=8, resid_done=8, xb_ready=8,
    k2_ready=1, k2_done=1, qk_ready=4, q_full=4, k1_done=2, q_split=4, v1_ready=3, v1_done=3,
    up_ready=4, gelu_done=8, g_hi=4, g_lo=4,
)
CREDIT = dict(resid_done=1, y_stored=1)


def decoder_kernel(nc, a, out):
    B, T, D = a["x"].shape
    DC = a["ctx_768"].shape[2]
    INNER = a["L0_xattn_Wq"].shape[1]
    DM = a["L1_xattn_mlp1_w"].shape[1]
    H = 16
    HD0, HD1 = INNER // H, D // H
    TURNS = B // PAIR
    TOK = PAIR * T
    KT = D // P
    DC1 = DC - P
    T0, T1, TM = INNER // P, D // P, DM // P
    GROUPS = PAIR * H // 4
    CK = [P, DC1]

    ctx = ExitStack()
    with ctx:
        def sb(name, shape, dt=F32, stack=ctx):
            return stack.enter_context(nc.sbuf_tensor(name, shape, dt))

        S = {n: ctx.enter_context(nc.semaphore(n)) for n in PER}
        S.update({n: ctx.enter_context(nc.semaphore(n)) for n in
                  ("w_hi_done", "w_lo_done", "params_loaded", "consts_built", "prep_steps", "prepared",
                   "params_turned", "ones_set", "raw_loaded")})
        w_loaded = [ctx.enter_context(nc.semaphore(f"w_loaded{n}")) for n in range(8)]

        def at(sem, i, k):
            return i * PER[sem] + k + CREDIT.get(sem, 0)

        def split_pair(name, shape):
            return sb(name + "_hi", shape, F32R), sb(name + "_lo", shape, F32R)

        WEIGHTS = [
            ("wk", a["L0_xattn_Wk"]), ("wv", a["L0_xattn_Wv"]), ("wq", a["L0_xattn_Wq"]), ("wo", a["L0_xattn_Wo"]),
            ("v1", a["L1_xattn_qkv_w"][:, 2 * D:3 * D]), ("mid", None), ("up", a["L1_xattn_mlp1_w"]), ("down", a["L1_xattn_mlp2_w"])]
        MID = [("k2", "L1_xattn_k_w"), ("v2", "L1_xattn_v_w"), ("pr", "L1_xattn_proj_w"), ("ou", "L1_xattn_out_w")]
        W = {}
        W["wk"] = split_pair("wk", [P, 2, INNER])
        W["wv"] = split_pair("wv", [P, 2, INNER])
        W["wq"] = split_pair("wq", [P, KT, INNER])
        W["wo"] = split_pair("wo", [P, T0, D])
        W["v1"] = split_pair("wv1", [P, KT, D])
        W["mid"] = split_pair("mid", [P, 2, 4 * D])
        wqk = sb("wqk", [P, KT, 2 * D])
        wq2 = sb("wq2", [P, KT, D])
        W["up"] = split_pair("up", [P, KT, DM])
        W["down"] = split_pair("down", [P, TM, D])
        MIDCOL = {n: D * i for i, (n, _) in enumerate(MID)}

        ident = sb("ident", [P, P])
        identb = sb("identb", [P, P], BF16)
        causal = sb("causal", [P, P], BF16)
        blocks = sb("blocks", [P, 8])
        qbias = sb("qbias", [P, 2, T1])
        minus_half = sb("minus_half", [P, PAIR])
        prow = sb("prow", [40, P])
        pcol = sb("pcol", [P, 40])
        COL, at_col = {}, 0
        for name, ap, n in (
                ("g0", a["L0_xattn_gamma"], KT), ("b0", a["L0_xattn_beta"], KT),
                ("g1", a["L1_xattn_ln1_w"], KT), ("b1", a["L1_xattn_ln1_b"], KT),
                ("g2", a["L1_xattn_ln2_w"], KT), ("b2", a["L1_xattn_ln2_b"], KT),
                ("g3", a["L1_xattn_ln3_w"], KT), ("b3", a["L1_xattn_ln3_b"], KT),
                ("qkvb", a["L1_xattn_qkv_b"], 3 * T1), ("qb", a["L1_xattn_q_b"], T1), ("kb", a["L1_xattn_k_b"], T1),
                ("vb", a["L1_xattn_v_b"], T1), ("upb", a["L1_xattn_mlp1_b"], TM)):
            COL[name] = (at_col, n, ap)
            at_col += n
        assert at_col <= 40
        brow = sb("brow", [P, 4, D])
        BROWS = [a["L0_xattn_bo"], a["L1_xattn_proj_b"], a["L1_xattn_out_b"], a["L1_xattn_mlp2_b"]]

        def col(name, t):
            return pcol[:, COL[name][0] + t:COL[name][0] + t + 1]

        x_in = sb("x_in", [P, PAIR, D])
        c_in = sb("c_in", [P, PAIR, DC])
        m_in = sb("m_in", [P, 2, PAIR, T], U8)
        mask_add = sb("mask_add", [P, 2, PAIR, T], BF16)
        xres = sb("xres", [P, PAIR, D])
        xb = sb("xb", [P, PAIR, D])
        wait_pad = sb("wait_pad", [P, 1])
        stats = sb("stats", [P, PAIR, 6])
        mv = sb("mv", [P, PAIR, 2])
        vare = sb("vare", [P, PAIR])
        rstd = sb("rstd", [P, PAIR])
        xhat = sb("xhat", [P, PAIR, D])
        h_h, h_l = split_pair("h", [P, KT, TOK])
        c_h, c_l = split_pair("cT", [P, 2, TOK])
        probs = sb("probs", [P, 3, 4, T])
        pts = sb("pts", [P, 2, 4, T])
        nmax = sb("nmax", [P, 4, 4])
        rec = sb("rec", [P, 2, H])
        o_n = sb("o_n", [P, 2, D])
        h_f = sb("h_f", [P, KT, TOK])

        k2 = sb("k2", [P, T1, TOK])
        v2 = sb("v2", [P, PAIR, H, HD1 + 1])
        with ExitStack() as stack:
            stage = sb("stage", [P, 4, 2 * INNER], stack=stack)
        with ExitStack() as stack:
            q0 = sb("q0", [P, T0, TOK], stack=stack)
            k0 = sb("k0", [P, T0, TOK], stack=stack)
            v0 = sb("v0", [P, PAIR, H, HD0 + 1], stack=stack)
            oT_h = sb("oT_hi", [P, T0, TOK], F32R, stack)
            oT_l = sb("oT_lo", [P, T0, TOK], F32R, stack)
        with ExitStack() as stack:
            q1 = sb("q1", [P, PAIR, T1, H // T1, T], stack=stack)
            qf = sb("qf", [P, PAIR, T1, T], stack=stack)
            k1 = sb("k1", [P, T1, TOK], stack=stack)
            v1 = sb("v1", [P, PAIR, H, HD1 + 1], stack=stack)
            o1T_h = sb("o1T_hi", [P, T1, TOK], F32R, stack)
            o1T_l = sb("o1T_lo", [P, T1, TOK], F32R, stack)
        with ExitStack() as stack:
            g_f = sb("g_f", [P, 2, 2, TOK], stack=stack)
            g_h = sb("g_hi", [P, TM, TOK], F32R, stack)
            g_l = sb("g_lo", [P, TM, TOK], F32R, stack)

        sc = [ctx.enter_context(nc.psum_tensor(f"sc{n}", [P, 4, T], F32)) for n in range(3)]
        pt = [ctx.enter_context(nc.psum_tensor(f"pt{n}", [P, 4, T], F32)) for n in range(2)]
        mb = [ctx.enter_context(nc.psum_tensor(f"mb{n}", [P, 512], F32)) for n in range(3)]

        USES, USE = [], {}

        def use(stage_name, n, sem, k):
            USE[stage_name, n] = len(USES)
            USES.append((sem, k))

        use("xhatT", 0, "h_full", 2)
        use("cT", 0, "c_lo", 2)
        for n in range(4):
            use("k0", n, "k0_done", n + 1)
        for n in range(4):
            use("v0", n, "v0_done", n + 1)
        for n in range(4):
            use("q0", n, "q0_done", n + 1)
        for s in range(LAG_PV, GROUPS + LAG_O):
            if s - LAG_PV < GROUPS:
                use("pv0", s - LAG_PV, "on_ready", s - LAG_PV + 1)
            if s >= LAG_O:
                use("oT0", s - LAG_O, "oT_lo", s - LAG_O + 1)
            if s == 8:
                use("resid", 0, "resid_done", 1)
            if s == 9:
                use("k2", 0, "k2_done", 1)
            if s == 10:
                use("v1", 0, "v1_done", 1)
            if s == 11:
                use("xhatT", 2, "h_full", 3)
        use("qk", 0, "k1_done", 1)
        use("v1", 1, "v1_done", 2)
        for att in (1, 2):
            use("resid", 2 * att - 1, "resid_done", 2 * att)
            use("xhatT", 2 * att + 1, "h_full", 2 * att + 2)
            use("pv%d" % att, 0, "on_ready", GROUPS + 2 * att - 1)
            use("qk", 2 * att - 1, *(("k1_done", 2) if att == 1 else ("q_full", 4)))
            if att == 1:
                use("v1", 2, "v1_done", 3)
            use("pv%d" % att, 1, "on_ready", GROUPS + 2 * att)
            use("oT%d" % att, 0, "oT_lo", GROUPS + 2 * att - 1)
            use("resid", 2 * att, "resid_done", 2 * att + 1)
            use("xhatT", 2 * att + 2, "h_full", 2 * att + 3)
            use("oT%d" % att, 1, "oT_lo", GROUPS + 2 * att)
            if att == 1:
                use("qk", 2, "q_full", 3)
        use("resid", 5, "resid_done", 6)
        use("xhatT", 7, "h_full", 8)
        for n in range(4):
            use("up", n, "gelu_done", 2 * n + 2)
        use("resid", 6, "resid_done", 7)
        use("resid", 7, "resid_done", 8)
        while len(USES) % 3:
            use("none", len(USES), "resid_done", 8)
        assert len(USES) % 3 == 0

        def bank(stage_name, n=0):
            return mb[USE[stage_name, n] % 3]

        def head0(g, j):
            gg, par = (g % 4) // 2, g % 2
            return 8 * gg + 2 * j + par

        def head1(g, j):
            return 4 * (g % 4) + j

        def v_bias(att, t):
            return col("qkvb", 2 * T1 + t) if att == 1 else col("vb", t)

        x_v = a["x"].rearrange("(i b) t d -> i t b d", b=PAIR)
        c_v = a["ctx_768"].rearrange("(i b) t d -> i t b d", b=PAIR)
        y_v = out.rearrange("(i b) t d -> i b t d", b=PAIR)
        m_v = [a[n].rearrange("(i b) t -> i b t", b=PAIR) for n in ("mask_BxS_bf0", "mask_BxS2_bf0")]

        def raw(name):
            slot = stage[:, [n for n, _ in WEIGHTS].index(name) % 4, :]
            if name in ("wk", "wv"):
                v = slot[:, 0:2 * INNER].rearrange("p (k n) -> p k n", k=2)
                w = dict(WEIGHTS)[name]
                return v, [(v[:, 0, :], w[0:P, :]), (v[0:DC1, 1, :], w[P:DC, :])]
            if name == "wo":
                v = slot[:, 0:T0 * D].rearrange("p (t n) -> p t n", t=T0)
                w = dict(WEIGHTS)[name].rearrange("(g j l r d) n -> g r l d j n", g=2, j=2, l=2, r=2)
                return v, [(v[HD0 * l:HD0 * l + HD0, 4 * g + 2 * r:4 * g + 2 * r + 2, :], w[g, r, l])
                           for g in range(2) for r in range(2) for l in range(2)]
            if name == "mid":
                v = slot.rearrange("p (k n) -> p k n", k=2)
                loads = []
                for n, full in MID:
                    c0 = MIDCOL[n]
                    w = a[full]
                    loads.append((v[:, 0, c0:c0 + D], w[0:P, :]))
                    rows = w.shape[0] - P
                    loads.append((v[0:rows, 1, c0:c0 + D], w[P:P + rows, :]))
                return v, loads
            w = dict(WEIGHTS)[name]
            k = w.shape[0] // P
            v = slot[:, 0:k * w.shape[1]].rearrange("p (k n) -> p k n", k=k)
            return v, [(v, w.rearrange("(k p) n -> p k n", p=P))]

        def pieces(name):
            if name in ("wk", "wv"):
                return [(P, slice(0, 1), slice(0, INNER)), (DC1, slice(1, 2), slice(0, INNER))]
            if name == "mid":
                return [(P, slice(0, 1), slice(0, 4 * D)), (DC1, slice(1, 2), slice(0, 2 * D)),
                        (P, slice(1, 2), slice(2 * D, 4 * D))]
            n = W[name][0].shape
            return [(P, slice(0, n[1]), slice(0, n[2]))]

        NPIECE = [0]
        for n, _ in WEIGHTS:
            NPIECE.append(NPIECE[-1] + len(pieces(n)))

        block = ctx.enter_context(nc.Block())

        @block.sync
        def _(sp):
            def load_turn(i):
                sp.dma_start(x_in[:], x_v[i]).then_inc(S["x_loaded"], 16)
                sp.dma_start(c_in[:], c_v[i]).then_inc(S["c_loaded"], 16)
                for m in range(2):
                    for b in range(PAIR):
                        sp.dma_start(m_in[:, m, b, :], m_v[m][i, b:b + 1, :].to_broadcast([P, T])) \
                          .then_inc(S["masks_loaded"], 16)

            def store_turn(i):
                for b in range(PAIR):
                    sp.wait_ge(S["resid_done"], at("resid_done", i, 7 + b))
                    sp.dma_start(y_v[i, b], xres[:, b, :]).then_inc(S["y_stored"], 16)

            load_turn(0)
            for n, (name, _) in enumerate(WEIGHTS):
                if n >= 4:
                    sp.wait_ge(S["w_lo_done"], NPIECE[n - 3])
                for dst, src in raw(name)[1]:
                    sp.dma_start(dst, src).then_inc(w_loaded[n], 16)
            sp.dma_start(wqk[:], a["L1_xattn_qkv_w"][:, 0:2 * D].rearrange("(k p) n -> p k n", p=P)) \
                .then_inc(S["raw_loaded"], 16)
            sp.dma_start(wq2[:], a["L1_xattn_q_w"].rearrange("(k p) n -> p k n", p=P)).then_inc(S["raw_loaded"], 16)
            with sp.Fori(1, TURNS) as i:
                sp.wait_ge(S["xhat_ready"], at("xhat_ready", i - 1, 2))
                sp.wait_ge(S["xb_ready"], at("xb_ready", i - 1, 2))
                sp.wait_ge(S["cT_ready"], at("cT_ready", i - 1, 1))
                sp.wait_ge(S["masks_ready"], at("masks_ready", i - 1, 2))
                load_turn(i)
                store_turn(i - 1)
            store_turn(TURNS - 1)
            sp.wait_ge(S["y_stored"], at("y_stored", TURNS, 0))

        @block.gpsimd
        def _(pool):
            nc.gpsimd.memset(ident[:], 0.0).then_inc(S["consts_built"], 1)
            nc.gpsimd.memset(causal[:], 0.0).then_inc(S["consts_built"], 1)
            nc.gpsimd.memset(blocks[:], 1.0).then_inc(S["consts_built"], 1)
            nc.gpsimd.memset(minus_half[:], -0.5).then_inc(S["consts_built"], 1)
            pool.wait_ge(S["consts_built"], 4)
            nc.gpsimd.affine_select(out=ident[:], in_=ident[:], compare_op=ALU.not_equal, fill=1.0, base=0,
                                    pattern=[[-1, P]], channel_multiplier=1).then_inc(S["consts_built"], 1)
            nc.gpsimd.affine_select(out=causal[:], in_=causal[:], compare_op=ALU.is_ge, fill=MASKED, base=0,
                                    pattern=[[-1, P]], channel_multiplier=1).then_inc(S["consts_built"], 1)
            nc.gpsimd.affine_select(out=blocks[:], in_=blocks[:], compare_op=ALU.is_ge, fill=0.0, base=0,
                                    pattern=[[-HD1, 8]], channel_multiplier=1).then_inc(S["consts_built"], 1)
            pool.wait_ge(S["consts_built"], 7)
            nc.gpsimd.affine_select(out=blocks[:], in_=blocks[:], compare_op=ALU.is_ge, fill=0.0, base=HD1 - 1,
                                    pattern=[[HD1, 8]], channel_multiplier=-1).then_inc(S["consts_built"], 1)
            for name, (c0, n, ap) in COL.items():
                pool.dma_start(prow[c0:c0 + n, :], ap.rearrange("(t p) -> t p", p=P)).then_inc(S["params_loaded"], 16)
            for n, ap in enumerate(BROWS):
                pool.dma_start(brow[:, n, :], ap.rearrange("(o d) -> o d", o=1).to_broadcast([P, D])) \
                    .then_inc(S["params_loaded"], 16)
            pool.wait_ge(S["params_loaded"], 16 * (len(COL) + len(BROWS)))

            def norm_scale(i, n, b):
                pool.wait_ge(S["ln_var"], at("ln_var", i, 2 * n + b + 1))
                nc.gpsimd.tensor_tensor(rstd[:, b:b + 1], vare[:, b:b + 1], minus_half[:, b:b + 1], ALU.pow) \
                    .then_inc(S["ln_rstd"], 1)

            def add_bias(i, n, b):
                src = x_in if n == 0 else xres
                if n == 0:
                    pool.wait_ge(S["x_loaded"], at("x_loaded", i, 16))
                    pool.wait_ge(S["resid_done"], at("resid_done", i, 0))
                else:
                    pool.wait_ge(S["resid_done"], at("resid_done", i, 2 * n - 1 + b))
                nc.gpsimd.tensor_tensor(xb[:, b, :], src[:, b, :], brow[:, n, :], ALU.add).then_inc(S["xb_ready"], 1)

            with pool.Fori(0, TURNS) as i:
                for n in range(4):
                    if n == 0:
                        norm_scale(i, 0, 0)
                        norm_scale(i, 0, 1)
                        add_bias(i, 0, 0)
                        add_bias(i, 0, 1)
                    else:
                        for b in range(PAIR):
                            norm_scale(i, n, b)
                            add_bias(i, n, b)

        @block.scalar
        def _(act):
            for n, (name, _) in enumerate(WEIGHTS):
                v, loads = raw(name)
                act.wait_ge(w_loaded[n], 16 * len(loads))
                for rows, k, c in pieces(name):
                    nc.scalar.activation(W[name][0][0:rows, k, c], v[0:rows, k, c], ACT.Copy) \
                        .then_inc(S["w_hi_done"], 1)
            act.wait_ge(S["prepared"], 1)
            act.wait_ge(S["w_lo_done"], NPIECE[-1])

            def h_high(i, n, b):
                act.wait_ge(S["h_full"], at("h_full", i, 2 * n + b + 1))
                nc.scalar.activation(h_h[:, :, b * T:(b + 1) * T], h_f[:, :, b * T:(b + 1) * T], ACT.Copy) \
                    .then_inc(S["h_hi"], 1)

            def step(i, att, s):
                base = att * GROUPS
                if s < GROUPS:
                    act.wait_ge(S["nmax_ready"], at("nmax_ready", i, base + s + 1))
                    for j in range(4):
                        e = nc.scalar.activation(probs[:, s % 3, j, :], sc[(base + s) % 3][:, j, :], ACT.Exp,
                                                 bias=nmax[:, (base + s) % 4, j:j + 1])
                    e.then_inc(S["exp_done"], 1)
                g = s - LAG_T
                if 0 <= g < GROUPS:
                    act.wait_ge(S["pt_ready"], at("pt_ready", i, base + g + 1))
                    if g >= 2:
                        act.wait_ge(S["pv_done"], at("pv_done", i, base + g - 1))
                    nc.scalar.activation(pts[:, g % 2], pt[g % 2][:], ACT.Copy).then_inc(S["pts_ready"], 1)
                g = s - LAG_O
                if att == 0 and 0 <= g < GROUPS:
                    act.wait_ge(S["oT_ready"], at("oT_ready", i, g + 1))
                    b, t = g // 4, 2 * (g % 4)
                    nc.scalar.activation(oT_h[:, t:t + 2, b * T:(b + 1) * T],
                                         bank("oT0", g)[:, 0:2 * T].rearrange("p (t c) -> p t c", t=2), ACT.Copy) \
                        .then_inc(S["oT_hi"], 1)

            def outT_high(i, att, b):
                act.wait_ge(S["oT_ready"], at("oT_ready", i, GROUPS + 2 * att - 1 + b))
                for t in range(T1):
                    o = nc.scalar.activation(o1T_h[:, t, b * T:(b + 1) * T], bank(f"oT{att}", b)[:, t * T:(t + 1) * T],
                                             ACT.Identity, bias=v_bias(att, t))
                o.then_inc(S["oT_hi"], 1)

            def queries(i, att, b):
                n = 2 * (att - 1) + b
                act.wait_ge(S["qk_ready"], at("qk_ready", i, n + 1))
                for t in range(T1):
                    q = nc.scalar.activation(qf[:, b, t, :], bank("qk", n)[:, t * T:(t + 1) * T], ACT.Identity,
                                             scale=float(HD1) ** -0.5, bias=qbias[:, att - 1, t:t + 1])
                q.then_inc(S["q_full"], 1)
                if att == 1:
                    for t in range(T1):
                        k = nc.scalar.activation(k1[:, t, b * T:(b + 1) * T],
                                                 bank("qk", n)[:, (T1 + t) * T:(T1 + t + 1) * T], ACT.Identity,
                                                 bias=col("qkvb", T1 + t))
                    k.then_inc(S["k1_done"], 1)

            with act.Fori(0, TURNS) as i:
                h_high(i, 0, 0)
                h_high(i, 0, 1)
                act.wait_ge(S["cT_ready"], at("cT_ready", i, 1))
                for k in range(2):
                    nc.scalar.activation(c_h[0:CK[k], k, :], bank("cT")[0:CK[k], k * TOK:(k + 1) * TOK], ACT.Copy) \
                        .then_inc(S["c_hi"], 1)
                for n in range(4):
                    act.wait_ge(S["k0_ready"], at("k0_ready", i, n + 1))
                    nc.scalar.activation(k0[:, 2 * n:2 * n + 2, :].rearrange("p t c -> p (t c)"), bank("k0", n)[:],
                                         ACT.Copy).then_inc(S["k0_done"], 1)
                for n in range(4):
                    act.wait_ge(S["q0_ready"], at("q0_ready", i, n + 1))
                    nc.scalar.activation(q0[:, 2 * n:2 * n + 2, :].rearrange("p t c -> p (t c)"), bank("q0", n)[:],
                                         ACT.Copy).then_inc(S["q0_done"], 1)
                for s in range(GROUPS + LAG_O):
                    step(i, 0, s)
                    if s == 10:
                        act.wait_ge(S["k2_ready"], at("k2_ready", i, 1))
                        for t in range(T1):
                            k = nc.scalar.activation(k2[:, t, :], bank("k2", 0)[:, t * TOK:(t + 1) * TOK], ACT.Identity,
                                                     bias=col("kb", t))
                        k.then_inc(S["k2_done"], 1)
                h_high(i, 1, 0)
                queries(i, 1, 0)
                for att in (1, 2):
                    for s in range(GROUPS + LAG_PV):
                        step(i, att, s)
                        if s == 2:
                            h_high(i, att, 1)
                        if s == 3:
                            queries(i, att, 1)
                        if s == 7:
                            outT_high(i, att, 0)
                        if s == 10:
                            h_high(i, att + 1, 0)
                    outT_high(i, att, 1)
                    if att == 1:
                        queries(i, 2, 0)
                h_high(i, 3, 1)
                for n in range(4):
                    act.wait_ge(S["up_ready"], at("up_ready", i, n + 1))
                    if n >= 2:
                        act.wait_ge(S["g_lo"], at("g_lo", i, n - 1))
                    for t in range(2):
                        nc.scalar.activation(g_f[:, n % 2, t, :], bank("up", n)[:, t * TOK:(t + 1) * TOK], ACT.Gelu,
                                             bias=col("upb", 2 * n + t)).then_inc(S["gelu_done"], 1)

        @block.vector
        def _(dve):
            for n, (name, _) in enumerate(WEIGHTS):
                v, loads = raw(name)
                for m, (rows, k, c) in enumerate(pieces(name)):
                    dve.wait_ge(S["w_hi_done"], NPIECE[n] + m + 1)
                    dve.wait_ge(w_loaded[n], 16 * len(loads))
                    nc.vector.tensor_tensor(W[name][1][0:rows, k, c], v[0:rows, k, c], W[name][0][0:rows, k, c],
                                            ALU.subtract).then_inc(S["w_lo_done"], 1)
            dve.wait_ge(S["consts_built"], 8)
            nc.vector.tensor_copy(identb[:], ident[:]).then_inc(S["prep_steps"], 1)
            dve.wait_ge(S["params_turned"], 1)
            nc.vector.tensor_copy(pcol[:, 0:at_col], sc[0][:, 0, 0:at_col]).then_inc(S["prep_steps"], 1)
            dve.wait_ge(S["prep_steps"], 2)
            for att, name in enumerate(("qkvb", "qb")):
                nc.vector.tensor_scalar(qbias[:, att, :], pcol[:, COL[name][0]:COL[name][0] + T1],
                                        float(HD1) ** -0.5, None, ALU.mult).then_inc(S["prep_steps"], 1)
            nc.vector.memset(v2[:, :, :, HD1:HD1 + 1], 1.0).then_inc(S["ones_set"], 1)
            dve.wait_ge(S["prep_steps"], 4)
            nc.vector.memset(wait_pad[:], 0.0).then_inc(S["resid_done"], CREDIT["resid_done"])
            nc.vector.memset(nmax[:], 0.0).then_inc(S["y_stored"], CREDIT["y_stored"])
            dve.wait_ge(S["resid_done"], 1)
            dve.wait_ge(S["y_stored"], 1)
            nc.vector.memset(o_n[:], 0.0).then_inc(S["prepared"], 1)
            dve.wait_ge(S["prepared"], 1)

            def norm(i, n, b):
                src = x_in if n == 0 else xres
                m = 2 * n + b
                if n == 0:
                    dve.wait_ge(S["x_loaded"], at("x_loaded", i, 16))
                else:
                    dve.wait_ge(S["resid_done"], at("resid_done", i, m - 1))
                nc.vector.bn_stats(stats[:, b, :], src[:, b, :]).then_inc(S["ln_stats"], 1)
                dve.wait_ge(S["ln_stats"], at("ln_stats", i, 2 * m + 1))
                nc.vector.memset(wait_pad[:], 0.0).then_inc(S["ln_stats"], 1)
                nc.vector.bn_aggr(mv[:, b, :], stats[:, b, :]).then_inc(S["ln_aggr"], 1)
                dve.wait_ge(S["ln_aggr"], at("ln_aggr", i, m + 1))
                nc.vector.tensor_scalar(vare[:, b:b + 1], mv[:, b, 1:2], EPS, None, ALU.add).then_inc(S["ln_var"], 1)

            def normalise(i, n, b):
                src = x_in if n == 0 else xres
                dve.wait_ge(S["ln_rstd"], at("ln_rstd", i, 2 * n + b + 1))
                nc.vector.tensor_scalar(xhat[:, b, :], src[:, b, :], mv[:, b, 0:1], rstd[:, b:b + 1],
                                        ALU.subtract, ALU.mult).then_inc(S["xhat_ready"], 1)

            def scale_shift(i, n, b):
                m = 2 * n + b
                dve.wait_ge(S["xhatT_ready"], at("xhatT_ready", i, m + 1 if n else 2))
                for k in range(KT):
                    c = (k * PAIR + b) * T if n == 0 else k * T
                    h = nc.vector.tensor_scalar(h_f[:, k, b * T:(b + 1) * T],
                                                bank("xhatT", m if n else 0)[:, c:c + T], col(f"g{n}", k),
                                                col(f"b{n}", k), ALU.mult, ALU.add)
                h.then_inc(S["h_full"], 1)

            def h_low(i, n, b):
                dve.wait_ge(S["h_full"], at("h_full", i, 2 * n + b + 1))
                dve.wait_ge(S["h_hi"], at("h_hi", i, 2 * n + b + 1))
                tok = slice(b * T, (b + 1) * T)
                nc.vector.tensor_tensor(h_l[:, :, tok], h_f[:, :, tok], h_h[:, :, tok], ALU.subtract) \
                    .then_inc(S["h_lo"], 1)

            def row_max(i, att, g):
                n = att * GROUPS + g
                dve.wait_ge(S["scores_ready"], at("scores_ready", i, n + 1))
                m = nmax[:, n % 4, :]
                r = nc.vector.tensor_reduce(m, sc[n % 3][:], AX, ALU.max, negate=True)
                if att == 0:
                    r.then_inc(S["nmax_ready"], 1)
                    return
                r.then_inc(S["raw_max"], 1)
                dve.wait_ge(S["raw_max"], at("raw_max", i, n - GROUPS + 1))
                nc.vector.tensor_scalar(m, m, 4.0, 0.25, ALU.mult, ALU.mult).then_inc(S["nmax_ready"], 1)

            def residual(i, n, b):
                m = 2 * n + b
                dve.wait_ge(S["resid_ready"], at("resid_ready", i, m + 1))
                dve.wait_ge(S["xb_ready"], at("xb_ready", i, m + 1))
                if n == 0:
                    dve.wait_ge(S["y_stored"], at("y_stored", i, 0))
                nc.vector.tensor_tensor(xres[:, b, :], bank("resid", m)[:, 0:D], xb[:, b, :], ALU.add) \
                    .then_inc(S["resid_done"], 1)

            def values(i, b):
                dve.wait_ge(S["v1_ready"], at("v1_ready", i, b + 2))
                nc.vector.tensor_copy(v1[:, b, :, 0:HD1], bank("v1", b + 1)[:, 0:D].rearrange("p (h d) -> p h d", h=H)) \
                    .then_inc(S["v1_done"], 1)

            def queries(i, att, b):
                n = 2 * (att - 1) + b
                dve.wait_ge(S["q_full"], at("q_full", i, n + 1))
                for t in range(T1):
                    q = nc.vector.tensor_tensor(q1[:, b, t], qf[:, b, t:t + 1, :].to_broadcast([P, H // T1, T]),
                                                blocks[:].unsqueeze(2).to_broadcast([P, H // T1, T]), ALU.mult)
                q.then_inc(S["q_split"], 1)

            def out_norm(i, att, b):
                dve.wait_ge(S["pv_done"], at("pv_done", i, att * GROUPS + 4 * b + 4))
                o = bank(f"pv{att}", b)[:, 0:H * (HD1 + 1)].rearrange("p (h d) -> p h d", h=H)
                nc.vector.reciprocal(rec[:, b, :], o[:, :, HD1]).then_inc(S["recip1"], 1)
                dve.wait_ge(S["recip1"], at("recip1", i, 2 * (att - 1) + b + 1))
                nc.vector.tensor_tensor(o_n[:, b, :].rearrange("p (h d) -> p h d", h=H), o[:, :, 0:HD1],
                                        rec[:, b, :].unsqueeze(2).to_broadcast([P, H, HD1]), ALU.mult) \
                    .then_inc(S["on_ready"], 1)

            def outT_low(i, att, b):
                dve.wait_ge(S["oT_hi"], at("oT_hi", i, GROUPS + 2 * att - 1 + b))
                for t in range(T1):
                    o = nc.vector.scalar_tensor_tensor(out=o1T_l[:, t, b * T:(b + 1) * T],
                                                       in0=bank(f"oT{att}", b)[:, t * T:(t + 1) * T],
                                                       scalar=v_bias(att, t), in1=o1T_h[:, t, b * T:(b + 1) * T],
                                                       op0=ALU.add, op1=ALU.subtract)
                o.then_inc(S["oT_lo"], 1)

            def out0(i, g):
                dve.wait_ge(S["pv_done"], at("pv_done", i, g + 1))
                o = bank("pv0", g)[:, 0:4 * (HD0 + 1)].rearrange("p (h d) -> p h d", h=4)
                r = rec[:, g % 2, 0:4]
                nc.vector.reciprocal(r, o[:, :, HD0]).then_inc(S["recip0"], 1)
                dve.wait_ge(S["recip0"], at("recip0", i, g + 1))
                nc.vector.scalar_tensor_tensor(out=o_n[:, g % 2, :].rearrange("p (h d) -> p h d", h=4),
                                               in0=o[:, :, 0:HD0], scalar=float(HD0) ** -0.5,
                                               in1=r.unsqueeze(2).to_broadcast([P, 4, HD0]),
                                               op0=ALU.mult, op1=ALU.mult).then_inc(S["on_ready"], 1)

            def oT0_low(i, g):
                dve.wait_ge(S["oT_hi"], at("oT_hi", i, g + 1))
                b, t = g // 4, 2 * (g % 4)
                nc.vector.tensor_tensor(oT_l[:, t:t + 2, b * T:(b + 1) * T],
                                        bank("oT0", g)[:, 0:2 * T].rearrange("p (t c) -> p t c", t=2),
                                        oT_h[:, t:t + 2, b * T:(b + 1) * T], ALU.subtract).then_inc(S["oT_lo"], 1)

            with dve.Fori(0, TURNS) as i:
                norm(i, 0, 0)
                norm(i, 0, 1)
                normalise(i, 0, 0)
                normalise(i, 0, 1)
                scale_shift(i, 0, 0)
                scale_shift(i, 0, 1)
                dve.wait_ge(S["masks_loaded"], at("masks_loaded", i, 64))
                nc.vector.scalar_tensor_tensor(out=mask_add[:, 0], in0=m_in[:, 0], scalar=MASKED,
                                               in1=causal[:, None, :].to_broadcast([P, PAIR, T]), op0=ALU.mult,
                                               op1=ALU.min).then_inc(S["masks_ready"], 1)
                nc.vector.tensor_scalar(mask_add[:, 1], m_in[:, 1], MASKED, None, ALU.mult) \
                    .then_inc(S["masks_ready"], 1)
                h_low(i, 0, 0)
                h_low(i, 0, 1)
                dve.wait_ge(S["c_hi"], at("c_hi", i, 2))
                for k in range(2):
                    nc.vector.tensor_tensor(c_l[0:CK[k], k, :], bank("cT")[0:CK[k], k * TOK:(k + 1) * TOK],
                                            c_h[0:CK[k], k, :], ALU.subtract).then_inc(S["c_lo"], 1)
                nc.vector.memset(v0[:, :, :, HD0:HD0 + 1], 1.0)
                for n in range(4):
                    dve.wait_ge(S["v0_ready"], at("v0_ready", i, n + 1))
                    nc.vector.tensor_copy(v0[:, n // 2, 8 * (n % 2):8 * (n % 2) + 8, 0:HD0],
                                          bank("v0", n)[:].rearrange("p (h d) -> p h d", h=8)).then_inc(S["v0_done"], 1)
                for s in range(GROUPS + LAG_O):
                    if s < GROUPS:
                        row_max(i, 0, s)
                    if 0 <= s - LAG_PV < GROUPS:
                        out0(i, s - LAG_PV)
                    if s >= LAG_O:
                        oT0_low(i, s - LAG_O)
                    if s == 8:
                        residual(i, 0, 0)
                        norm(i, 1, 0)
                    if s == 9:
                        normalise(i, 1, 0)
                    if s == 10:
                        dve.wait_ge(S["v1_ready"], at("v1_ready", i, 1))
                        nc.vector.tensor_copy(v2[:, :, :, 0:HD1],
                                              bank("v1", 0)[:].rearrange("p (b h d) -> p b h d", b=PAIR, h=H)) \
                            .then_inc(S["v1_done"], 1)
                scale_shift(i, 1, 0)
                h_low(i, 1, 0)
                nc.vector.memset(v1[:, :, :, HD1:HD1 + 1], 1.0)
                queries(i, 1, 0)
                values(i, 0)
                for att in (1, 2):
                    for s in range(GROUPS + LAG_PV):
                        if s < GROUPS:
                            row_max(i, att, s)
                        if s == 0:
                            residual(i, att - 1, 1)
                            norm(i, att, 1)
                        if s == 1:
                            normalise(i, att, 1)
                        if s == 2:
                            scale_shift(i, att, 1)
                            h_low(i, att, 1)
                        if s == 3:
                            queries(i, att, 1)
                            if att == 1:
                                values(i, 1)
                        if s == 6:
                            out_norm(i, att, 0)
                        if s == 7:
                            outT_low(i, att, 0)
                        if s == 8:
                            residual(i, att, 0)
                            norm(i, att + 1, 0)
                        if s == 9:
                            normalise(i, att + 1, 0)
                        if s == 10:
                            out_norm(i, att, 1)
                            scale_shift(i, att + 1, 0)
                            h_low(i, att + 1, 0)
                    outT_low(i, att, 1)
                    if att == 1:
                        queries(i, 2, 0)
                residual(i, 2, 1)
                norm(i, 3, 1)
                normalise(i, 3, 1)
                scale_shift(i, 3, 1)
                h_low(i, 3, 1)
                for n in range(4):
                    dve.wait_ge(S["gelu_done"], at("gelu_done", i, 2 * n + 2))
                    nc.vector.tensor_copy(g_h[:, 2 * n:2 * n + 2, :], g_f[:, n % 2]).then_inc(S["g_hi"], 1)
                    dve.wait_ge(S["g_hi"], at("g_hi", i, n + 1))
                    nc.vector.tensor_tensor(g_l[:, 2 * n:2 * n + 2, :], g_f[:, n % 2], g_h[:, 2 * n:2 * n + 2, :],
                                            ALU.subtract).then_inc(S["g_lo"], 1)
                residual(i, 3, 0)
                residual(i, 3, 1)

        @block.tensor
        def _(pe):
            pe.wait_ge(S["consts_built"], 8)
            pe.wait_ge(S["params_loaded"], 16 * (len(COL) + len(BROWS)))
            nc.tensor.transpose(sc[0][:, 0, 0:at_col], prow[0:at_col, :], ident[0:at_col, 0:at_col]) \
                .then_inc(S["params_turned"], 1)
            pe.wait_ge(S["w_lo_done"], NPIECE[-1])
            pe.wait_ge(S["prepared"], 1)
            pe.wait_ge(S["raw_loaded"], 32)

            used = [0]

            def free(i, stage_name, n=0):
                u = USE[stage_name, n]
                assert u == used[0], (stage_name, n)
                used[0] += 1
                if u >= 3:
                    sem, k = USES[u - 3]
                    pe.wait_ge(S[sem], at(sem, i, k))

            def product(dst, lhs, rhs, first=True, last=True):
                n = len(lhs)
                for k in range(n):
                    for p, (l, r) in enumerate(((0, 0), (0, 1), (1, 0))):
                        m = nc.tensor.matmul(dst, lhs[k][l], rhs[k][r], start=(first and k == 0 and p == 0),
                                             stop=(last and k == n - 1 and p == 2))
                return m

            def w_tiles(name, rows, c0, cols):
                return [(W[name][0][0:r, k, c0:c0 + cols], W[name][1][0:r, k, c0:c0 + cols])
                        for k, r in enumerate(rows)]

            def a_tiles(pair, rows, c0, cols):
                return [(pair[0][0:r, k, c0:c0 + cols], pair[1][0:r, k, c0:c0 + cols]) for k, r in enumerate(rows)]

            FULL = [P] * KT

            def feature_major(i, stage_name, n, sem, name, c0, src, rows, tiles=2):
                free(i, stage_name, n)
                for t in range(tiles):
                    m = product(bank(stage_name, n)[:, t * TOK:(t + 1) * TOK],
                                w_tiles(name, rows, c0 + t * P, P), a_tiles(src, rows, 0, TOK))
                m.then_inc(S[sem], 1)

            def sequence(i, stage_name, n, sem, name, c0, src, rows, b):
                free(i, stage_name, n)
                product(bank(stage_name, n)[:, 0:D], a_tiles(src, rows, b * T, T), w_tiles(name, rows, c0, D)) \
                    .then_inc(S[sem], 1)

            def transpose_norm(i, n, b):
                m = 2 * n + b
                if n or not b:
                    free(i, "xhatT", m)
                pe.wait_ge(S["xhat_ready"], at("xhat_ready", i, m + 1))
                for k in range(KT):
                    c = (k * PAIR + b) * T if n == 0 else k * T
                    t = nc.tensor.transpose(bank("xhatT", m if n else 0)[:, c:c + T], xhat[:, b, k * P:(k + 1) * P],
                                            ident[:])
                t.then_inc(S["xhatT_ready"], 1)

            def queries(i, att, b):
                n = 2 * (att - 1) + b
                free(i, "qk", n)
                pe.wait_ge(S["h_full"], at("h_full", i, 2 * att + b + 1))
                w = wqk if att == 1 else wq2
                for t in range(2 * T1 if att == 1 else T1):
                    for k in range(KT):
                        m = nc.tensor.matmul(bank("qk", n)[:, t * T:(t + 1) * T], w[:, k, t * P:(t + 1) * P],
                                             h_f[:, k, b * T:(b + 1) * T], start=(k == 0), stop=(k == KT - 1))
                m.then_inc(S["qk_ready"], 1)

            def values(i, b):
                pe.wait_ge(S["h_lo"], at("h_lo", i, 2 + b + 1))
                sequence(i, "v1", b + 1, "v1_ready", "v1", 0, (h_h, h_l), FULL, b)

            def attended(i, att, b):
                n = 2 * att + b
                if att == 0:
                    pe.wait_ge(S["oT_lo"], at("oT_lo", i, 4 * b + 4))
                    sequence(i, "resid", n, "resid_ready", "wo", 0, (oT_h, oT_l), [P] * T0, b)
                else:
                    pe.wait_ge(S["oT_lo"], at("oT_lo", i, GROUPS + n - 1))
                    sequence(i, "resid", n, "resid_ready", "mid", MIDCOL["pr" if att == 1 else "ou"],
                             (o1T_h, o1T_l), FULL, b)

            def score(i, att, g):
                n = att * GROUPS + g
                b = g // 4
                dst = sc[n % 3]
                tok = slice(b * T, (b + 1) * T)
                if att == 0:
                    for j in range(4):
                        h = head0(g, j)
                        r = slice(HD0 * (h % 2), HD0 * (h % 2) + HD0)
                        m = nc.tensor.matmul(dst[:, j, :], q0[r, h // 2, tok], k0[r, h // 2, tok], start=True, stop=True)
                else:
                    if g % 4 == 0:
                        pe.wait_ge(S["q_split"], at("q_split", i, 2 * (att - 1) + b + 1))
                        if att == 1:
                            pe.wait_ge(S["k1_done"], at("k1_done", i, b + 1))
                    keys = k1 if att == 1 else k2
                    nc.tensor.matmul(dst[:], identb[:], mask_add[:, att - 1, b:b + 1, :].to_broadcast([P, 4, T]),
                                     start=True, stop=False)
                    for j in range(4):
                        t, h = divmod(head1(g, j), H // T1)
                        m = nc.tensor.matmul(dst[:, j, :], q1[:, b, t, h, :], keys[:, t, tok], start=False, stop=(j == 3))
                m.then_inc(S["scores_ready"], 1)

            def turn_probs(i, att, g):
                n = att * GROUPS + g
                pe.wait_ge(S["exp_done"], at("exp_done", i, n + 1))
                for j in range(4):
                    m = nc.tensor.transpose(pt[g % 2][:, j, :], probs[:, g % 3, j, :], ident[:])
                m.then_inc(S["pt_ready"], 1)

            def weigh(i, att, g):
                n, b = att * GROUPS + g, g // 4
                if att == 0:
                    free(i, "pv0", g)
                elif g % 4 == 0:
                    free(i, f"pv{att}", b)
                if att == 1 and g % 4 == 0:
                    pe.wait_ge(S["v1_done"], at("v1_done", i, b + 2))
                pe.wait_ge(S["pts_ready"], at("pts_ready", i, n + 1))
                for j in range(4):
                    if att == 0:
                        dst = bank("pv0", g)[:, j * (HD0 + 1):(j + 1) * (HD0 + 1)]
                        v = v0[:, b, head0(g, j), :]
                    else:
                        h = head1(g, j)
                        dst = bank(f"pv{att}", b)[:, h * (HD1 + 1):(h + 1) * (HD1 + 1)]
                        v = (v1 if att == 1 else v2)[:, b, h, :]
                    m = nc.tensor.matmul(dst, pts[:, g % 2, j, :], v, start=True, stop=True)
                m.then_inc(S["pv_done"], 1)

            def turn_out0(i, g):
                free(i, "oT0", g)
                pe.wait_ge(S["on_ready"], at("on_ready", i, g + 1))
                for k in range(2):
                    m = nc.tensor.transpose(bank("oT0", g)[:, k * P:(k + 1) * P], o_n[:, g % 2, k * P:(k + 1) * P],
                                            ident[:])
                m.then_inc(S["oT_ready"], 1)

            def turn_out1(i, att, b):
                free(i, f"oT{att}", b)
                pe.wait_ge(S["on_ready"], at("on_ready", i, GROUPS + 2 * att - 1 + b))
                for k in range(T1):
                    m = nc.tensor.transpose(bank(f"oT{att}", b)[:, k * T:(k + 1) * T], o_n[:, b, k * P:(k + 1) * P],
                                            ident[:])
                m.then_inc(S["oT_ready"], 1)

            def step(i, att, s):
                if s < GROUPS:
                    score(i, att, s)
                if 0 <= s - LAG_T < GROUPS:
                    turn_probs(i, att, s - LAG_T)
                if 0 <= s - LAG_PV < GROUPS:
                    weigh(i, att, s - LAG_PV)
                if att == 0 and s >= LAG_O:
                    turn_out0(i, s - LAG_O)

            with pe.Fori(0, TURNS) as i:
                pe.wait_ge(S["resid_done"], at("resid_done", i, 0))
                transpose_norm(i, 0, 0)
                transpose_norm(i, 0, 1)
                free(i, "cT")
                pe.wait_ge(S["c_loaded"], at("c_loaded", i, 16))
                for b in range(PAIR):
                    for k in range(2):
                        m = nc.tensor.transpose(bank("cT")[0:CK[k], k * TOK + b * T:k * TOK + (b + 1) * T],
                                                c_in[:, b, k * P:k * P + CK[k]], ident[:])
                m.then_inc(S["cT_ready"], 1)
                pe.wait_ge(S["c_lo"], at("c_lo", i, 2))
                for n in range(4):
                    feature_major(i, "k0", n, "k0_ready", "wk", 2 * P * n, (c_h, c_l), CK)
                for n in range(4):
                    free(i, "v0", n)
                    product(bank("v0", n)[:], a_tiles((c_h, c_l), CK, (n // 2) * T, T),
                            w_tiles("wv", CK, 512 * (n % 2), 512)).then_inc(S["v0_ready"], 1)
                pe.wait_ge(S["h_lo"], at("h_lo", i, 2))
                for n in range(4):
                    feature_major(i, "q0", n, "q0_ready", "wq", 2 * P * n, (h_h, h_l), FULL)
                pe.wait_ge(S["q0_done"], at("q0_done", i, 4))
                pe.wait_ge(S["v0_done"], at("v0_done", i, 4))
                for s in range(GROUPS + LAG_O):
                    step(i, 0, s)
                    if s == 8:
                        attended(i, 0, 0)
                    if s == 9:
                        feature_major(i, "k2", 0, "k2_ready", "mid", MIDCOL["k2"], (c_h, c_l), CK)
                    if s == 10:
                        free(i, "v1", 0)
                        for b in range(PAIR):
                            m = product(bank("v1", 0)[:, b * D:(b + 1) * D], a_tiles((c_h, c_l), CK, b * T, T),
                                        w_tiles("mid", CK, MIDCOL["v2"], D))
                        m.then_inc(S["v1_ready"], 1)
                    if s == 11:
                        transpose_norm(i, 1, 0)
                queries(i, 1, 0)
                values(i, 0)
                pe.wait_ge(S["masks_ready"], at("masks_ready", i, 2))
                for att in (1, 2):
                    for s in range(GROUPS + LAG_PV):
                        step(i, att, s)
                        if s == 0:
                            attended(i, att - 1, 1)
                        if s == 2:
                            transpose_norm(i, att, 1)
                        if s == 3:
                            queries(i, att, 1)
                            if att == 1:
                                values(i, 1)
                        if s == 7:
                            turn_out1(i, att, 0)
                        if s == 8:
                            attended(i, att, 0)
                        if s == 10:
                            transpose_norm(i, att + 1, 0)
                    turn_out1(i, att, 1)
                    if att == 1:
                        queries(i, 2, 0)
                        pe.wait_ge(S["k2_done"], at("k2_done", i, 1))
                attended(i, 2, 1)
                transpose_norm(i, 3, 1)
                pe.wait_ge(S["h_lo"], at("h_lo", i, 8))
                for n in range(4):
                    feature_major(i, "up", n, "up_ready", "up", 2 * P * n, (h_h, h_l), FULL)
                free(i, "resid", 6)
                free(i, "resid", 7)
                for n in range(4):
                    pe.wait_ge(S["g_lo"], at("g_lo", i, n + 1))
                    for b in range(PAIR):
                        m = product(bank("resid", 6 + b)[:, 0:D],
                                    [(g_h[:, k, b * T:(b + 1) * T], g_l[:, k, b * T:(b + 1) * T])
                                     for k in (2 * n, 2 * n + 1)],
                                    [(W["down"][0][:, k, :], W["down"][1][:, k, :]) for k in (2 * n, 2 * n + 1)],
                                    first=(n == 0), last=(n == 3))
                        if n == 3:
                            m.then_inc(S["resid_ready"], 1)


_OUT = ((32, 128, 256), 'float32')


def kernel(**inputs):
    import numpy as _np
    import concourse.bacc as _bacc
    from concourse import mybir as _mybir
    from concourse.bass_utils import run_bass_kernel_spmd as _run

    nc = _bacc.Bacc("TRN2", target_bir_lowering=False, num_devices=1)
    arrays, args = {}, {}
    for name, value in inputs.items():
        x = _np.ascontiguousarray(value)
        arrays[f"in_{name}_dram"] = x
        args[name] = nc.dram_tensor(f"in_{name}_dram", x.shape, _mybir.dt.from_np(x.dtype), kind="ExternalInput").ap()
    out = nc.dram_tensor("out_0_dram", _OUT[0], _mybir.dt.float32, kind="ExternalOutput").ap()
    decoder_kernel(nc, args, out)
    r = _run(nc, [arrays], core_ids=[0])
    return r.results[0]["out_0_dram"]
```

```python
from contextlib import ExitStack

import concourse.bass as bass
from concourse import mybir

F32 = mybir.dt.float32
F32R = mybir.dt.float32r
BF16 = mybir.dt.bfloat16
U8 = mybir.dt.uint8
ALU = mybir.AluOpType
ACT = mybir.ActivationFunctionType
AX = mybir.AxisListType.X

P = 128
PAIR = 2
EPS = 1e-5
MASKED = -3.0e38
LAG_T, LAG_PV, LAG_O = 2, 3, 4

PER = dict(
    x_loaded=16, c_loaded=16, masks_loaded=64, y_stored=32,
    ln_stats=16, ln_aggr=8, ln_var=8, ln_rstd=8, xhat_ready=8, xhatT_ready=8, h_full=8, h_hi=6, h_lo=6,
    cT_ready=1, c_hi=2, c_lo=2, masks_ready=2,
    k0_ready=4, k0_done=4, v0_ready=4, v0_done=4, q0_ready=4, q0_done=4,
    scores_ready=24, raw_max=16, nmax_ready=24, exp_done=24, pt_ready=24, pts_ready=24, pv_done=24,
    recip0=8, on_ready=12, recip1=4, oT_ready=12, oT_hi=12, oT_lo=12,
    resid_ready=8, resid_done=8, xb_ready=8,
    k2_ready=1, k2_done=1, qk_ready=4, q_full=4, k1_done=2, q_split=8, q_split_late=8, v1_ready=3, v1_done=3,
    up_ready=4, gelu_done=8, g_hi=4, g_lo=4,
)
CREDIT = dict(resid_done=2, y_stored=1)


def decoder_kernel(nc, a, out):
    B, T, D = a["x"].shape
    DC = a["ctx_768"].shape[2]
    INNER = a["L0_xattn_Wq"].shape[1]
    DM = a["L1_xattn_mlp1_w"].shape[1]
    H = 16
    HD0, HD1 = INNER // H, D // H
    TURNS = B // PAIR
    TOK = PAIR * T
    KT = D // P
    DC1 = DC - P
    T0, T1, TM = INNER // P, D // P, DM // P
    GROUPS = PAIR * H // 4
    CK = [P, DC1]

    ctx = ExitStack()
    with ctx:
        def sb(name, shape, dt=F32, stack=ctx):
            return stack.enter_context(nc.sbuf_tensor(name, shape, dt))

        S = {n: ctx.enter_context(nc.semaphore(n)) for n in PER}
        S.update({n: ctx.enter_context(nc.semaphore(n)) for n in
                  ("w_hi_done", "w_lo_done", "params_loaded", "consts_built", "prep_steps", "prepared",
                   "params_turned", "raw_loaded")})
        w_loaded = [ctx.enter_context(nc.semaphore(f"w_loaded{n}")) for n in range(8)]

        def at(sem, i, k):
            return i * PER[sem] + k + CREDIT.get(sem, 0)

        PRE, MORE, LAST = range(3)

        def norm_at(sem, i, n, b, mode):
            split = sem in ("h_hi", "h_lo")
            each = PER[sem] // (6 if split else 8)
            if mode == PRE:
                return each * (b + 1)
            order = [m for m in (1, 2, 0, 3) if not (m == 0 and mode == LAST) and not (m == 2 and split)]
            return i * PER[sem] + each * (2 + 2 * order.index(n) + b + 1)

        def split_pair(name, shape):
            return sb(name + "_hi", shape, F32R), sb(name + "_lo", shape, F32R)

        WEIGHTS = [
            ("wk", a["L0_xattn_Wk"]), ("wv", a["L0_xattn_Wv"]), ("wq", a["L0_xattn_Wq"]), ("wo", a["L0_xattn_Wo"]),
            ("v1", a["L1_xattn_qkv_w"][:, 2 * D:3 * D]), ("mid", None), ("up", a["L1_xattn_mlp1_w"]), ("down", a["L1_xattn_mlp2_w"])]
        MID = [("k2", "L1_xattn_k_w"), ("v2", "L1_xattn_v_w"), ("pr", "L1_xattn_proj_w"), ("ou", "L1_xattn_out_w")]
        W = {}
        W["wk"] = split_pair("wk", [P, 2, INNER])
        W["wv"] = split_pair("wv", [P, 2, INNER])
        W["wq"] = split_pair("wq", [P, KT, INNER])
        W["wo"] = split_pair("wo", [P, T0, D])
        W["v1"] = split_pair("wv1", [P, KT, D])
        W["mid"] = split_pair("mid", [P, 2, 4 * D])
        wqk = sb("wqk", [P, KT, 2 * D])
        wq2 = sb("wq2", [P, KT, D])
        W["up"] = split_pair("up", [P, KT, DM])
        W["down"] = split_pair("down", [P, TM, D])
        MIDCOL = {n: D * i for i, (n, _) in enumerate(MID)}

        ident = sb("ident", [P, P])
        identb = sb("identb", [P, P], BF16)
        causal = sb("causal", [P, P], BF16)
        blocks = sb("blocks", [P, 8])
        qbias = sb("qbias", [P, 2, T1])
        minus_half = sb("minus_half", [P, PAIR])
        prow = sb("prow", [40, P])
        pcol = sb("pcol", [P, 40])
        COL, at_col = {}, 0
        for name, ap, n in (
                ("g0", a["L0_xattn_gamma"], KT), ("b0", a["L0_xattn_beta"], KT),
                ("g1", a["L1_xattn_ln1_w"], KT), ("b1", a["L1_xattn_ln1_b"], KT),
                ("g2", a["L1_xattn_ln2_w"], KT), ("b2", a["L1_xattn_ln2_b"], KT),
                ("g3", a["L1_xattn_ln3_w"], KT), ("b3", a["L1_xattn_ln3_b"], KT),
                ("qkvb", a["L1_xattn_qkv_b"], 3 * T1), ("qb", a["L1_xattn_q_b"], T1), ("kb", a["L1_xattn_k_b"], T1),
                ("vb", a["L1_xattn_v_b"], T1), ("upb", a["L1_xattn_mlp1_b"], TM)):
            COL[name] = (at_col, n, ap)
            at_col += n
        assert at_col <= 40
        brow = sb("brow", [P, 4, D])
        BROWS = [a["L0_xattn_bo"], a["L1_xattn_proj_b"], a["L1_xattn_out_b"], a["L1_xattn_mlp2_b"]]

        def col(name, t):
            return pcol[:, COL[name][0] + t:COL[name][0] + t + 1]

        x_in = sb("x_in", [P, PAIR, D])
        c_in = sb("c_in", [P, PAIR, DC])
        m_in = sb("m_in", [P, 2, PAIR, T], U8)
        mask_add = sb("mask_add", [P, 2, PAIR, T], BF16)
        xres = sb("xres", [P, PAIR, D])
        xb = sb("xb", [P, PAIR, D])
        wait_pad = sb("wait_pad", [P, 1])
        stats = sb("stats", [P, PAIR, 6])
        mv = sb("mv", [P, PAIR, 2])
        vare = sb("vare", [P, PAIR])
        rstd = sb("rstd", [P, PAIR])
        xhat = sb("xhat", [P, PAIR, D])
        h_h, h_l = split_pair("h", [P, KT, TOK])
        c_h, c_l = split_pair("cT", [P, 2, TOK])
        probs = sb("probs", [P, 3, 4, T])
        pts = sb("pts", [P, 2, 4, T])
        nmax = sb("nmax", [P, 4, 4])
        rec = sb("rec", [P, 2, H])
        o_n = sb("o_n", [P, 2, D])
        h_f = sb("h_f", [P, KT, TOK])

        k2 = sb("k2", [P, T1, TOK])
        v2 = sb("v2", [P, PAIR, H, HD1 + 1])
        with ExitStack() as stack:
            stage = sb("stage", [P, 4, 2 * INNER], stack=stack)
        with ExitStack() as stack:
            k0 = sb("k0", [P, T0, TOK], stack=stack)
            v0 = sb("v0", [P, PAIR, H, HD0 + 1], stack=stack)
            q0 = sb("q0", [P, T0, TOK], stack=stack)
            oT_h = sb("oT_hi", [P, T0, TOK], F32R, stack)
            oT_l = sb("oT_lo", [P, T0, TOK], F32R, stack)
        with ExitStack() as stack:
            q1 = sb("q1", [P, PAIR, T1, H // T1, T], stack=stack)
            qf = sb("qf", [P, PAIR, T1, T], stack=stack)
            k1 = sb("k1", [P, T1, TOK], stack=stack)
            v1 = sb("v1", [P, PAIR, H, HD1 + 1], stack=stack)
            o1T_h = sb("o1T_hi", [P, T1, TOK], F32R, stack)
            o1T_l = sb("o1T_lo", [P, T1, TOK], F32R, stack)
        with ExitStack() as stack:
            sb("k0v0", [P, T0 * TOK + PAIR * H * (HD0 + 1)], stack=stack)
            g_f = sb("g_f", [P, 2, 2, TOK], stack=stack)
            g_h = sb("g_hi", [P, TM, TOK], F32R, stack)
            g_l = sb("g_lo", [P, TM, TOK], F32R, stack)
            x0_h = sb("x0_hi", [P, KT, TOK], F32R, stack)
            x0_l = sb("x0_lo", [P, KT, TOK], F32R, stack)
        x0_f = g_f[:, 0]
        x0_hat = g_f[:, 1]

        sc = [ctx.enter_context(nc.psum_tensor(f"sc{n}", [P, 4, T], F32)) for n in range(3)]
        pt = [ctx.enter_context(nc.psum_tensor(f"pt{n}", [P, 4, T], F32)) for n in range(2)]
        sc_banks = [t[:].rearrange("p h k -> p (h k)") for t in sc]
        mb = [ctx.enter_context(nc.psum_tensor(f"mb{n}", [P, 512], F32)) for n in range(3)]

        USES, USE = [], {}

        last_bank = [2]

        def use(stage_name, n, sem, k, ahead=0, skip=0, spare=None):
            USE[stage_name, n] = len(USES)
            if spare is None:
                last_bank[0] = (last_bank[0] + 1 + skip) % 3
                USES.append((sem, k, ahead, last_bank[0]))
            else:
                USES.append((sem, k, ahead, 3 + GROUPS * (spare + 1) % 3))

        for n in range(4):
            use("q0", n, "q0_done", n + 1)
        for s in range(LAG_PV, GROUPS + LAG_O):
            if LAG_O <= s < GROUPS:
                use("oT0", s - LAG_O, "oT_lo", s - LAG_O + 1)
            if s == 8:
                use("resid", 0, "resid_done", 1, spare=0)
            if s == 10:
                use("xhatT", 2, "h_full", (1, 0), spare=0)
            if s == 11:
                use("qk", 0, "k1_done", 1)
            if s - LAG_PV < GROUPS:
                use("pv0", s - LAG_PV, "on_ready", s - LAG_PV + 1)
            if s >= GROUPS:
                use("oT0", s - LAG_O, "oT_lo", s - LAG_O + 1)
        use("v1", 0, "v1_done", 1)
        use("resid", 1, "resid_done", 2, skip=1)
        use("xhatT", 3, "h_full", (1, 1))
        use("qk", 1, "k1_done", 2)
        use("pv1", 0, "on_ready", GROUPS + 1)
        use("v1", 1, "v1_done", 2)
        use("oT1", 0, "oT_lo", GROUPS + 1)
        use("pv1", 1, "on_ready", GROUPS + 2)
        use("resid", 2, "resid_done", 3, spare=1)
        use("k2", 0, "k2_done", 1)
        use("xhatT", 4, "h_full", (2, 0), spare=1)
        use("qk", 2, "q_full", 3)
        use("oT1", 1, "oT_lo", GROUPS + 2)
        use("v2", 0, "v1_done", 3)
        use("resid", 3, "resid_done", 4)
        use("xhatT", 5, "h_full", (2, 1))
        use("qk", 3, "q_full", 4)
        use("pv2", 0, "on_ready", GROUPS + 3)
        use("cT", 0, "c_lo", 2, 1)
        use("xhatT", 0, "h_full", (0, 1), 1)
        use("oT2", 0, "oT_lo", GROUPS + 3)
        use("pv2", 1, "on_ready", GROUPS + 4)
        use("resid", 4, "resid_done", 5, spare=2)
        use("k0", 0, "k0_done", 1, 1, skip=1)
        use("xhatT", 6, "h_full", (3, 0), spare=2)
        use("k0", 1, "k0_done", 2, 1, skip=1)
        use("oT2", 1, "oT_lo", GROUPS + 4)
        use("k0", 2, "k0_done", 3, 1)
        use("k0", 3, "k0_done", 4, 1)
        use("resid", 5, "resid_done", 6, spare=2)
        use("v0", 0, "v0_done", 1, 1)
        use("v0", 1, "v0_done", 2, 1)
        use("xhatT", 7, "h_full", (3, 1), spare=2)
        use("v0", 2, "v0_done", 3, 1)
        use("v0", 3, "v0_done", 4, 1)
        use("up", 0, "gelu_done", 2, skip=-(last_bank[0] + 1) % 3)
        for n in range(1, 4):
            use("up", n, "gelu_done", 2 * n + 2)
        use("resid", 6, "resid_done", 7)
        use("resid", 7, "resid_done", 8)
        assert USES[-1][3] == 2

        def bank(stage_name, n=0):
            return (mb + sc_banks)[USES[USE[stage_name, n]][3]]

        def head0(g, j):
            gg, par = (g % 4) // 2, g % 2
            return 8 * gg + 2 * j + par

        def head1(g, j):
            return 4 * (g % 4) + j

        def mask_queries(b, g):
            t, h = divmod(4 * g, H // T1)
            return (q1[:, b, t, h:h + 4, :], qf[:, b, t:t + 1, :].to_broadcast([P, 4, T]),
                    blocks[:, h:h + 4].unsqueeze(2).to_broadcast([P, 4, T]))

        def v_bias(att, t):
            return col("qkvb", 2 * T1 + t) if att == 1 else col("vb", t)

        x_v = a["x"].rearrange("(i b) t d -> i t b d", b=PAIR)
        c_v = a["ctx_768"].rearrange("(i b) t d -> i t b d", b=PAIR)
        y_v = out.rearrange("(i b) t d -> i b t d", b=PAIR)
        m_v = [a[n].rearrange("(i b) t -> i b t", b=PAIR) for n in ("mask_BxS_bf0", "mask_BxS2_bf0")]

        def raw(name):
            slot = stage[:, [n for n, _ in WEIGHTS].index(name) % 4, :]
            if name in ("wk", "wv"):
                v = slot[:, 0:2 * INNER].rearrange("p (k n) -> p k n", k=2)
                w = dict(WEIGHTS)[name]
                return v, [(v[:, 0, :], w[0:P, :]), (v[0:DC1, 1, :], w[P:DC, :])]
            if name == "wo":
                v = slot[:, 0:T0 * D].rearrange("p (t n) -> p t n", t=T0)
                w = dict(WEIGHTS)[name].rearrange("(g j l r d) n -> g r l d j n", g=2, j=2, l=2, r=2)
                return v, [(v[HD0 * l:HD0 * l + HD0, 4 * g + 2 * r:4 * g + 2 * r + 2, :], w[g, r, l])
                           for g in range(2) for r in range(2) for l in range(2)]
            if name == "mid":
                v = slot.rearrange("p (k n) -> p k n", k=2)
                loads = []
                for n, full in MID:
                    c0 = MIDCOL[n]
                    w = a[full]
                    loads.append((v[:, 0, c0:c0 + D], w[0:P, :]))
                    rows = w.shape[0] - P
                    loads.append((v[0:rows, 1, c0:c0 + D], w[P:P + rows, :]))
                return v, loads
            w = dict(WEIGHTS)[name]
            k = w.shape[0] // P
            v = slot[:, 0:k * w.shape[1]].rearrange("p (k n) -> p k n", k=k)
            return v, [(v, w.rearrange("(k p) n -> p k n", p=P))]

        def pieces(name):
            if name in ("wk", "wv"):
                return [(P, slice(0, 1), slice(0, INNER)), (DC1, slice(1, 2), slice(0, INNER))]
            if name == "mid":
                return [(P, slice(0, 1), slice(0, 4 * D)), (DC1, slice(1, 2), slice(0, 2 * D)),
                        (P, slice(1, 2), slice(2 * D, 4 * D))]
            n = W[name][0].shape
            return [(P, slice(0, n[1]), slice(0, n[2]))]

        NPIECE = [0]
        for n, _ in WEIGHTS:
            NPIECE.append(NPIECE[-1] + len(pieces(n)))

        block = ctx.enter_context(nc.Block())

        @block.sync
        def _(sp):
            def load_turn(i):
                sp.dma_start(x_in[:], x_v[i]).then_inc(S["x_loaded"], 16)
                sp.dma_start(c_in[:], c_v[i]).then_inc(S["c_loaded"], 16)
                for m in range(2):
                    for b in range(PAIR):
                        sp.dma_start(m_in[:, m, b, :], m_v[m][i, b:b + 1, :].to_broadcast([P, T])) \
                          .then_inc(S["masks_loaded"], 16)

            def store_turn(i):
                for b in range(PAIR):
                    sp.wait_ge(S["resid_done"], at("resid_done", i, 7 + b))
                    sp.dma_start(y_v[i, b], xres[:, b, :]).then_inc(S["y_stored"], 16)

            load_turn(0)
            for n, (name, _) in enumerate(WEIGHTS):
                if n >= 4:
                    sp.wait_ge(S["w_lo_done"], NPIECE[n - 3])
                for dst, src in raw(name)[1]:
                    sp.dma_start(dst, src).then_inc(w_loaded[n], 16)
            sp.dma_start(wqk[:], a["L1_xattn_qkv_w"][:, 0:2 * D].rearrange("(k p) n -> p k n", p=P)) \
                .then_inc(S["raw_loaded"], 16)
            sp.dma_start(wq2[:], a["L1_xattn_q_w"].rearrange("(k p) n -> p k n", p=P)).then_inc(S["raw_loaded"], 16)
            with sp.Fori(1, TURNS) as i:
                sp.wait_ge(S["xhat_ready"], at("xhat_ready", i - 1, 2))
                sp.wait_ge(S["xb_ready"], at("xb_ready", i - 1, 2))
                sp.wait_ge(S["cT_ready"], at("cT_ready", i - 1, 1))
                sp.wait_ge(S["masks_ready"], at("masks_ready", i - 1, 2))
                load_turn(i)
                store_turn(i - 1)
            store_turn(TURNS - 1)
            sp.wait_ge(S["y_stored"], at("y_stored", TURNS, 0))

        @block.gpsimd
        def _(pool):
            nc.gpsimd.memset(ident[:], 0.0).then_inc(S["consts_built"], 1)
            nc.gpsimd.memset(causal[:], 0.0).then_inc(S["consts_built"], 1)
            nc.gpsimd.memset(blocks[:], 1.0).then_inc(S["consts_built"], 1)
            nc.gpsimd.memset(minus_half[:], -0.5).then_inc(S["consts_built"], 1)
            pool.wait_ge(S["consts_built"], 4)
            nc.gpsimd.affine_select(out=ident[:], in_=ident[:], compare_op=ALU.not_equal, fill=1.0, base=0,
                                    pattern=[[-1, P]], channel_multiplier=1).then_inc(S["consts_built"], 1)
            nc.gpsimd.affine_select(out=causal[:], in_=causal[:], compare_op=ALU.is_ge, fill=MASKED, base=0,
                                    pattern=[[-1, P]], channel_multiplier=1).then_inc(S["consts_built"], 1)
            nc.gpsimd.affine_select(out=blocks[:], in_=blocks[:], compare_op=ALU.is_ge, fill=0.0, base=0,
                                    pattern=[[-HD1, 8]], channel_multiplier=1).then_inc(S["consts_built"], 1)
            pool.wait_ge(S["consts_built"], 7)
            nc.gpsimd.affine_select(out=blocks[:], in_=blocks[:], compare_op=ALU.is_ge, fill=0.0, base=HD1 - 1,
                                    pattern=[[HD1, 8]], channel_multiplier=-1).then_inc(S["consts_built"], 1)
            pool.wait_ge(S["consts_built"], 8)
            for name, (c0, n, ap) in COL.items():
                pool.dma_start(prow[c0:c0 + n, :], ap.rearrange("(t p) -> t p", p=P)).then_inc(S["params_loaded"], 16)
            for n, ap in enumerate(BROWS):
                pool.dma_start(brow[:, n, :], ap.rearrange("(o d) -> o d", o=1).to_broadcast([P, D])) \
                    .then_inc(S["params_loaded"], 16)
            pool.wait_ge(S["params_loaded"], 16 * (len(COL) + len(BROWS)))

            def norm_scale(i, n, b, mode):
                pool.wait_ge(S["ln_var"], norm_at("ln_var", i, n, b, mode))
                nc.gpsimd.tensor_tensor(rstd[:, b:b + 1], vare[:, b:b + 1], minus_half[:, b:b + 1], ALU.pow) \
                    .then_inc(S["ln_rstd"], 1)

            def add_bias(i, n, b):
                src = x_in if n == 0 else xres
                if n == 0:
                    pool.wait_ge(S["x_loaded"], at("x_loaded", i, 16))
                    pool.wait_ge(S["resid_done"], at("resid_done", i, 0))
                else:
                    pool.wait_ge(S["resid_done"], at("resid_done", i, 2 * n - 1 + b))
                nc.gpsimd.tensor_tensor(xb[:, b, :], src[:, b, :], brow[:, n, :], ALU.add).then_inc(S["xb_ready"], 1)

            def queries(i, att, b):
                pool.wait_ge(S["q_full"], at("q_full", i, 2 * (att - 1) + b + 1))
                for g in (2, 3):
                    nc.gpsimd.tensor_tensor(*mask_queries(b, g), ALU.mult).then_inc(S["q_split_late"], 1)

            def turn(i, mode):
                add_bias(i, 0, 0)
                add_bias(i, 0, 1)
                for n in range(1, 4):
                    if n == 3 and mode == MORE:
                        for b in range(PAIR):
                            norm_scale(i, 0, b, mode)
                    for b in range(PAIR):
                        norm_scale(i, n, b, mode)
                        add_bias(i, n, b)
                        if n < 3:
                            queries(i, n, b)

            for b in range(PAIR):
                norm_scale(0, 0, b, PRE)
            with pool.Fori(0, TURNS - 1) as i:
                turn(i, MORE)
            turn(TURNS - 1, LAST)

        @block.scalar
        def _(act):
            def h_high(i, n, b, mode):
                act.wait_ge(S["h_full"], norm_at("h_full", i, n, b, mode))
                tok = slice(b * T, (b + 1) * T)
                dst, src = (x0_h, x0_f) if n == 0 else (h_h, h_f)
                nc.scalar.activation(dst[:, :, tok], src[:, :, tok], ACT.Copy).then_inc(S["h_hi"], 1)

            def context_high(j):
                act.wait_ge(S["cT_ready"], at("cT_ready", j, 1))
                for k in range(2):
                    nc.scalar.activation(c_h[0:CK[k], k, :], bank("cT")[0:CK[k], k * TOK:(k + 1) * TOK], ACT.Copy) \
                        .then_inc(S["c_hi"], 1)

            def keys0(j, n):
                act.wait_ge(S["k0_ready"], at("k0_ready", j, n + 1))
                nc.scalar.activation(k0[:, 2 * n:2 * n + 2, :].rearrange("p t c -> p (t c)"), bank("k0", n)[:],
                                     ACT.Copy).then_inc(S["k0_done"], 1)

            def keys2(i):
                act.wait_ge(S["k2_ready"], at("k2_ready", i, 1))
                for t in range(T1):
                    k = nc.scalar.activation(k2[:, t, :], bank("k2", 0)[:, t * TOK:(t + 1) * TOK], ACT.Identity,
                                             bias=col("kb", t))
                k.then_inc(S["k2_done"], 1)

            def outT0_high(i, g):
                act.wait_ge(S["oT_ready"], at("oT_ready", i, g + 1))
                b, t = g // 4, 2 * (g % 4)
                nc.scalar.activation(oT_h[:, t:t + 2, b * T:(b + 1) * T],
                                     bank("oT0", g)[:, 0:2 * T].rearrange("p (t c) -> p t c", t=2), ACT.Copy) \
                    .then_inc(S["oT_hi"], 1)

            def step(i, att, s):
                base = att * GROUPS
                g = s - LAG_O
                if att == 0 and 0 <= g < GROUPS - LAG_O:
                    outT0_high(i, g)
                g = s - LAG_T
                if 0 <= g < GROUPS:
                    act.wait_ge(S["pt_ready"], at("pt_ready", i, base + g + 1))
                    if g >= 2:
                        act.wait_ge(S["pv_done"], at("pv_done", i, base + g - 1))
                    nc.scalar.activation(pts[:, g % 2], pt[g % 2][:], ACT.Copy).then_inc(S["pts_ready"], 1)
                if s < GROUPS:
                    act.wait_ge(S["nmax_ready"], at("nmax_ready", i, base + s + 1))
                    for j in range(4):
                        e = nc.scalar.activation(probs[:, s % 3, j, :], sc[(base + s) % 3][:, j, :], ACT.Exp,
                                                 bias=nmax[:, (base + s) % 4, j:j + 1])
                    e.then_inc(S["exp_done"], 1)
                g = s - LAG_O
                if att == 0 and GROUPS - LAG_O <= g < GROUPS:
                    outT0_high(i, g)

            def outT_high(i, att, b):
                act.wait_ge(S["oT_ready"], at("oT_ready", i, GROUPS + 2 * att - 1 + b))
                for t in range(T1):
                    o = nc.scalar.activation(o1T_h[:, t, b * T:(b + 1) * T], bank(f"oT{att}", b)[:, t * T:(t + 1) * T],
                                             ACT.Identity, bias=v_bias(att, t))
                o.then_inc(S["oT_hi"], 1)

            def queries(i, att, b):
                n = 2 * (att - 1) + b
                act.wait_ge(S["qk_ready"], at("qk_ready", i, n + 1))
                for t in range(T1):
                    q = nc.scalar.activation(qf[:, b, t, :], bank("qk", n)[:, t * T:(t + 1) * T], ACT.Identity,
                                             scale=float(HD1) ** -0.5, bias=qbias[:, att - 1, t:t + 1])
                q.then_inc(S["q_full"], 1)
                if att == 1:
                    for t in range(T1):
                        k = nc.scalar.activation(k1[:, t, b * T:(b + 1) * T],
                                                 bank("qk", n)[:, (T1 + t) * T:(T1 + t + 1) * T], ACT.Identity,
                                                 bias=col("qkvb", T1 + t))
                    k.then_inc(S["k1_done"], 1)

            def turn(i, mode):
                for n in range(4):
                    act.wait_ge(S["q0_ready"], at("q0_ready", i, n + 1))
                    nc.scalar.activation(q0[:, 2 * n:2 * n + 2, :].rearrange("p t c -> p (t c)"), bank("q0", n)[:],
                                         ACT.Copy).then_inc(S["q0_done"], 1)
                for s in range(GROUPS + LAG_O):
                    step(i, 0, s)
                    if s == 10:
                        h_high(i, 1, 0, mode)
                queries(i, 1, 0)
                for att in (1, 2):
                    for s in range(GROUPS + LAG_PV):
                        if s == 3:
                            queries(i, att, 1)
                        if s == 7:
                            outT_high(i, att, 0)
                        step(i, att, s)
                        if s == 2 and att == 1:
                            h_high(i, att, 1, mode)
                        if s == 5 and att == 2 and mode == MORE:
                            context_high(i + 1)
                        if s == 9 and att == 2 and mode == MORE:
                            h_high(i, 0, 0, mode)
                            h_high(i, 0, 1, mode)
                        if s == 8:
                            if att == 1:
                                keys2(i)
                            elif mode == MORE:
                                keys0(i + 1, 0)
                        if s == 10:
                            if att == 1:
                                queries(i, 2, 0)
                            else:
                                h_high(i, 3, 0, mode)
                                if mode == MORE:
                                    keys0(i + 1, 1)
                    outT_high(i, att, 1)
                if mode == MORE:
                    keys0(i + 1, 2)
                    keys0(i + 1, 3)
                h_high(i, 3, 1, mode)
                for n in range(4):
                    act.wait_ge(S["up_ready"], at("up_ready", i, n + 1))
                    if n >= 2:
                        act.wait_ge(S["g_lo"], at("g_lo", i, n - 1))
                    for t in range(2):
                        nc.scalar.activation(g_f[:, n % 2, t, :], bank("up", n)[:, t * TOK:(t + 1) * TOK], ACT.Gelu,
                                             bias=col("upb", 2 * n + t)).then_inc(S["gelu_done"], 1)

            context_high(0)
            for n, (name, _) in enumerate(WEIGHTS):
                v, loads = raw(name)
                act.wait_ge(w_loaded[n], 16 * len(loads))
                for rows, k, c in pieces(name):
                    nc.scalar.activation(W[name][0][0:rows, k, c], v[0:rows, k, c], ACT.Copy) \
                        .then_inc(S["w_hi_done"], 1)
            act.wait_ge(S["prepared"], 1)
            act.wait_ge(S["w_lo_done"], NPIECE[-1])

            h_high(0, 0, 0, PRE)
            h_high(0, 0, 1, PRE)
            for n in range(4):
                keys0(0, n)
            with act.Fori(0, TURNS - 1) as i:
                turn(i, MORE)
            turn(TURNS - 1, LAST)

        @block.vector
        def _(dve):
            def norm(i, n, b, mode):
                src = x_in if n == 0 else xres
                if n == 0:
                    dve.wait_ge(S["x_loaded"], at("x_loaded", i + 1 if mode == MORE else 0, 16))
                else:
                    dve.wait_ge(S["resid_done"], at("resid_done", i, 2 * n - 1 + b))
                nc.vector.bn_stats(stats[:, b, :], src[:, b, :]).then_inc(S["ln_stats"], 1)
                dve.wait_ge(S["ln_stats"], norm_at("ln_stats", i, n, b, mode) - 1)
                nc.vector.memset(wait_pad[:], 0.0).then_inc(S["ln_stats"], 1)
                nc.vector.bn_aggr(mv[:, b, :], stats[:, b, :]).then_inc(S["ln_aggr"], 1)
                dve.wait_ge(S["ln_aggr"], norm_at("ln_aggr", i, n, b, mode))
                nc.vector.tensor_scalar(vare[:, b:b + 1], mv[:, b, 1:2], EPS, None, ALU.add).then_inc(S["ln_var"], 1)

            def normalise(i, n, b, mode):
                src = x_in if n == 0 else xres
                dst = x0_hat if n == 0 else xhat
                dve.wait_ge(S["ln_rstd"], norm_at("ln_rstd", i, n, b, mode))
                nc.vector.tensor_scalar(dst[:, b, :], src[:, b, :], mv[:, b, 0:1], rstd[:, b:b + 1],
                                        ALU.subtract, ALU.mult).then_inc(S["xhat_ready"], 1)

            def scale_shift(i, n, b, mode):
                dve.wait_ge(S["xhatT_ready"], norm_at("xhatT_ready", i, n, b if n else 1, mode))
                dst = x0_f if n == 0 else h_f
                for k in range(KT):
                    c = (k * PAIR + b) * T if n == 0 else k * T
                    h = nc.vector.tensor_scalar(dst[:, k, b * T:(b + 1) * T],
                                                bank("xhatT", 2 * n + b if n else 0)[:, c:c + T], col(f"g{n}", k),
                                                col(f"b{n}", k), ALU.mult, ALU.add)
                h.then_inc(S["h_full"], 1)

            def h_low(i, n, b, mode):
                dve.wait_ge(S["h_full"], norm_at("h_full", i, n, b, mode))
                dve.wait_ge(S["h_hi"], norm_at("h_hi", i, n, b, mode))
                tok = slice(b * T, (b + 1) * T)
                whole, hi, lo = (x0_f, x0_h, x0_l) if n == 0 else (h_f, h_h, h_l)
                nc.vector.tensor_tensor(lo[:, :, tok], whole[:, :, tok], hi[:, :, tok], ALU.subtract) \
                    .then_inc(S["h_lo"], 1)

            def context_low(j):
                dve.wait_ge(S["c_hi"], at("c_hi", j, 2))
                for k in range(2):
                    nc.vector.tensor_tensor(c_l[0:CK[k], k, :], bank("cT")[0:CK[k], k * TOK:(k + 1) * TOK],
                                            c_h[0:CK[k], k, :], ALU.subtract).then_inc(S["c_lo"], 1)

            def values0(j, n):
                if n == 0:
                    nc.vector.memset(v0[:, :, :, HD0:HD0 + 1], 1.0)
                dve.wait_ge(S["v0_ready"], at("v0_ready", j, n + 1))
                nc.vector.tensor_copy(v0[:, n // 2, 8 * (n % 2):8 * (n % 2) + 8, 0:HD0],
                                      bank("v0", n)[:].rearrange("p (h d) -> p h d", h=8)).then_inc(S["v0_done"], 1)

            def row_max(i, att, g):
                n = att * GROUPS + g
                dve.wait_ge(S["scores_ready"], at("scores_ready", i, n + 1))
                m = nmax[:, n % 4, :]
                r = nc.vector.tensor_reduce(m, sc[n % 3][:], AX, ALU.max, negate=True)
                if att == 0:
                    r.then_inc(S["nmax_ready"], 1)
                    return
                r.then_inc(S["raw_max"], 1)
                dve.wait_ge(S["raw_max"], at("raw_max", i, n - GROUPS + 1))
                nc.vector.tensor_scalar(m, m, 4.0, 0.25, ALU.mult, ALU.mult).then_inc(S["nmax_ready"], 1)

            def residual(i, n, b):
                m = 2 * n + b
                dve.wait_ge(S["resid_ready"], at("resid_ready", i, m + 1))
                dve.wait_ge(S["xb_ready"], at("xb_ready", i, m + 1))
                if n == 0:
                    dve.wait_ge(S["y_stored"], at("y_stored", i, 0))
                nc.vector.tensor_tensor(xres[:, b, :], bank("resid", m)[:, 0:D], xb[:, b, :], ALU.add) \
                    .then_inc(S["resid_done"], 1)

            def values(i, b):
                dve.wait_ge(S["v1_ready"], at("v1_ready", i, b + 1))
                nc.vector.tensor_copy(v1[:, b, :, 0:HD1], bank("v1", b)[:, 0:D].rearrange("p (h d) -> p h d", h=H)) \
                    .then_inc(S["v1_done"], 1)

            def queries(i, att, b, g):
                n = 2 * (att - 1) + b
                dve.wait_ge(S["q_full"], at("q_full", i, n + 1))
                nc.vector.tensor_tensor(*mask_queries(b, g), ALU.mult).then_inc(S["q_split"], 1)

            def out_norm(i, att, b):
                dve.wait_ge(S["pv_done"], at("pv_done", i, att * GROUPS + 4 * b + 4))
                o = bank(f"pv{att}", b)[:, 0:H * (HD1 + 1)].rearrange("p (h d) -> p h d", h=H)
                nc.vector.reciprocal(rec[:, b, :], o[:, :, HD1]).then_inc(S["recip1"], 1)
                dve.wait_ge(S["recip1"], at("recip1", i, 2 * (att - 1) + b + 1))
                nc.vector.tensor_tensor(o_n[:, b, :].rearrange("p (h d) -> p h d", h=H), o[:, :, 0:HD1],
                                        rec[:, b, :].unsqueeze(2).to_broadcast([P, H, HD1]), ALU.mult) \
                    .then_inc(S["on_ready"], 1)

            def outT_low(i, att, b):
                dve.wait_ge(S["oT_hi"], at("oT_hi", i, GROUPS + 2 * att - 1 + b))
                for t in range(T1):
                    o = nc.vector.scalar_tensor_tensor(out=o1T_l[:, t, b * T:(b + 1) * T],
                                                       in0=bank(f"oT{att}", b)[:, t * T:(t + 1) * T],
                                                       scalar=v_bias(att, t), in1=o1T_h[:, t, b * T:(b + 1) * T],
                                                       op0=ALU.add, op1=ALU.subtract)
                o.then_inc(S["oT_lo"], 1)

            def out0(i, g):
                dve.wait_ge(S["pv_done"], at("pv_done", i, g + 1))
                o = bank("pv0", g)[:, 0:4 * (HD0 + 1)].rearrange("p (h d) -> p h d", h=4)
                r = rec[:, g % 2, 0:4]
                nc.vector.reciprocal(r, o[:, :, HD0]).then_inc(S["recip0"], 1)
                dve.wait_ge(S["recip0"], at("recip0", i, g + 1))
                nc.vector.scalar_tensor_tensor(out=o_n[:, g % 2, :].rearrange("p (h d) -> p h d", h=4),
                                               in0=o[:, :, 0:HD0], scalar=float(HD0) ** -0.5,
                                               in1=r.unsqueeze(2).to_broadcast([P, 4, HD0]),
                                               op0=ALU.mult, op1=ALU.mult).then_inc(S["on_ready"], 1)

            def oT0_low(i, g):
                dve.wait_ge(S["oT_hi"], at("oT_hi", i, g + 1))
                b, t = g // 4, 2 * (g % 4)
                nc.vector.tensor_tensor(oT_l[:, t:t + 2, b * T:(b + 1) * T],
                                        bank("oT0", g)[:, 0:2 * T].rearrange("p (t c) -> p t c", t=2),
                                        oT_h[:, t:t + 2, b * T:(b + 1) * T], ALU.subtract).then_inc(S["oT_lo"], 1)

            def turn(i, mode):
                dve.wait_ge(S["masks_loaded"], at("masks_loaded", i, 64))
                nc.vector.scalar_tensor_tensor(out=mask_add[:, 0], in0=m_in[:, 0], scalar=MASKED,
                                               in1=causal[:, None, :].to_broadcast([P, PAIR, T]), op0=ALU.mult,
                                               op1=ALU.min).then_inc(S["masks_ready"], 1)
                nc.vector.tensor_scalar(mask_add[:, 1], m_in[:, 1], MASKED, None, ALU.mult) \
                    .then_inc(S["masks_ready"], 1)
                for s in range(GROUPS + LAG_O):
                    if LAG_O <= s <= GROUPS:
                        out0(i, s - LAG_O)
                    if s < GROUPS:
                        row_max(i, 0, s)
                    if s == 8:
                        residual(i, 0, 0)
                        norm(i, 1, 0, mode)
                    if s == 9:
                        normalise(i, 1, 0, mode)
                    if s == 10:
                        scale_shift(i, 1, 0, mode)
                    if s == 11:
                        h_low(i, 1, 0, mode)
                    if GROUPS <= s < GROUPS + LAG_PV:
                        out0(i, s - LAG_PV)
                    if s >= LAG_O:
                        oT0_low(i, s - LAG_O)
                nc.vector.memset(v1[:, :, :, HD1:HD1 + 1], 1.0)
                queries(i, 1, 0, 0)
                queries(i, 1, 0, 1)
                values(i, 0)
                residual(i, 0, 1)
                norm(i, 1, 1, mode)
                for att in (1, 2):
                    for s in range(GROUPS + LAG_PV):
                        if s < GROUPS:
                            row_max(i, att, s)
                        if s == 0 and att == 2:
                            residual(i, 1, 1)
                            norm(i, 2, 1, mode)
                        if s == att - 1:
                            normalise(i, att, 1, mode)
                        if s == 2:
                            scale_shift(i, att, 1, mode)
                            if att == 1:
                                h_low(i, att, 1, mode)
                        if s == 3:
                            queries(i, att, 1, 0)
                            queries(i, att, 1, 1)
                        if s == 4 and att == 1:
                            values(i, 1)
                        if att == 2 and mode == MORE:
                            if s == 4:
                                norm(i, 0, 0, mode)
                                norm(i, 0, 1, mode)
                            if s == 5:
                                normalise(i, 0, 0, mode)
                                normalise(i, 0, 1, mode)
                            if s == 6:
                                context_low(i + 1)
                        if s == 6:
                            out_norm(i, att, 0)
                        if s == 7:
                            outT_low(i, att, 0)
                            if att == 2 and mode == MORE:
                                scale_shift(i, 0, 0, mode)
                        if s == 8:
                            residual(i, att, 0)
                            norm(i, att + 1, 0, mode)
                            if att == 2 and mode == MORE:
                                scale_shift(i, 0, 1, mode)
                        if s == 9:
                            normalise(i, att + 1, 0, mode)
                            if att == 2 and mode == MORE:
                                h_low(i, 0, 0, mode)
                                h_low(i, 0, 1, mode)
                        if s == 10:
                            scale_shift(i, att + 1, 0, mode)
                            out_norm(i, att, 1)
                            if att == 2:
                                h_low(i, 3, 0, mode)
                            else:
                                queries(i, 2, 0, 0)
                    outT_low(i, att, 1)
                    if att == 1:
                        queries(i, 2, 0, 1)
                        dve.wait_ge(S["v1_ready"], at("v1_ready", i, 3))
                        nc.vector.tensor_copy(v2[:, :, :, 0:HD1],
                                              bank("v2")[:].rearrange("p (b h d) -> p b h d", b=PAIR, h=H)) \
                            .then_inc(S["v1_done"], 1)
                residual(i, 2, 1)
                norm(i, 3, 1, mode)
                normalise(i, 3, 1, mode)
                if mode == MORE:
                    values0(i + 1, 0)
                    values0(i + 1, 1)
                scale_shift(i, 3, 1, mode)
                if mode == MORE:
                    values0(i + 1, 2)
                h_low(i, 3, 1, mode)
                if mode == MORE:
                    values0(i + 1, 3)
                for n in range(4):
                    dve.wait_ge(S["gelu_done"], at("gelu_done", i, 2 * n + 2))
                    nc.vector.tensor_copy(g_h[:, 2 * n:2 * n + 2, :], g_f[:, n % 2]).then_inc(S["g_hi"], 1)
                    dve.wait_ge(S["g_hi"], at("g_hi", i, n + 1))
                    nc.vector.tensor_tensor(g_l[:, 2 * n:2 * n + 2, :], g_f[:, n % 2], g_h[:, 2 * n:2 * n + 2, :],
                                            ALU.subtract).then_inc(S["g_lo"], 1)
                residual(i, 3, 0)
                residual(i, 3, 1)

            for b in range(PAIR):
                norm(0, 0, b, PRE)
            context_low(0)
            for n, (name, _) in enumerate(WEIGHTS):
                v, loads = raw(name)
                for m, (rows, k, c) in enumerate(pieces(name)):
                    dve.wait_ge(S["w_hi_done"], NPIECE[n] + m + 1)
                    dve.wait_ge(w_loaded[n], 16 * len(loads))
                    nc.vector.tensor_tensor(W[name][1][0:rows, k, c], v[0:rows, k, c], W[name][0][0:rows, k, c],
                                            ALU.subtract).then_inc(S["w_lo_done"], 1)
            dve.wait_ge(S["consts_built"], 8)
            nc.vector.tensor_copy(identb[:], ident[:]).then_inc(S["prep_steps"], 1)
            dve.wait_ge(S["params_turned"], 1)
            nc.vector.tensor_copy(pcol[:, 0:at_col], sc[0][:, 0, 0:at_col]).then_inc(S["prep_steps"], 1)
            dve.wait_ge(S["prep_steps"], 2)
            for att, name in enumerate(("qkvb", "qb")):
                nc.vector.tensor_scalar(qbias[:, att, :], pcol[:, COL[name][0]:COL[name][0] + T1],
                                        float(HD1) ** -0.5, None, ALU.mult).then_inc(S["prep_steps"], 1)
            nc.vector.memset(v2[:, :, :, HD1:HD1 + 1], 1.0)
            dve.wait_ge(S["prep_steps"], 4)
            nc.vector.memset(wait_pad[:], 0.0).then_inc(S["resid_done"], CREDIT["resid_done"])
            nc.vector.memset(nmax[:], 0.0).then_inc(S["y_stored"], CREDIT["y_stored"])
            dve.wait_ge(S["resid_done"], 1)
            dve.wait_ge(S["y_stored"], 1)
            nc.vector.memset(o_n[:], 0.0).then_inc(S["prepared"], 1)
            dve.wait_ge(S["prepared"], 1)

            for b in range(PAIR):
                normalise(0, 0, b, PRE)
            for b in range(PAIR):
                scale_shift(0, 0, b, PRE)
            for b in range(PAIR):
                h_low(0, 0, b, PRE)
            for n in range(4):
                values0(0, n)
            with dve.Fori(0, TURNS - 1) as i:
                turn(i, MORE)
            turn(TURNS - 1, LAST)

        @block.tensor
        def _(pe):
            used = [0]

            def free(i, stage_name, n, mode):
                u = USE[stage_name, n]
                assert mode == PRE or u >= used[0], (stage_name, n)
                used[0] = u
                for p in range(u - 1, -1, -1):
                    sem, k, ahead, at_bank = USES[p]
                    if at_bank != USES[u][3] or (mode == PRE and not ahead) or (mode == LAST and ahead):
                        continue
                    if isinstance(k, tuple):
                        pe.wait_ge(S[sem], norm_at(sem, i, *k, mode))
                    else:
                        pe.wait_ge(S[sem], at(sem, i + 1 if ahead and mode == MORE else i, k))
                    return

            def product(dst, lhs, rhs, first=True, last=True):
                n = len(lhs)
                for k in range(n):
                    for p, (l, r) in enumerate(((0, 0), (0, 1), (1, 0))):
                        m = nc.tensor.matmul(dst, lhs[k][l], rhs[k][r], start=(first and k == 0 and p == 0),
                                             stop=(last and k == n - 1 and p == 2))
                return m

            def w_tiles(name, rows, c0, cols):
                return [(W[name][0][0:r, k, c0:c0 + cols], W[name][1][0:r, k, c0:c0 + cols])
                        for k, r in enumerate(rows)]

            def a_tiles(pair, rows, c0, cols):
                return [(pair[0][0:r, k, c0:c0 + cols], pair[1][0:r, k, c0:c0 + cols]) for k, r in enumerate(rows)]

            FULL = [P] * KT

            def feature_major(i, stage_name, n, sem, name, c0, src, rows, mode):
                free(i, stage_name, n, mode)
                for t in range(2):
                    m = product(bank(stage_name, n)[:, t * TOK:(t + 1) * TOK],
                                w_tiles(name, rows, c0 + t * P, P), a_tiles(src, rows, 0, TOK))
                m.then_inc(S[sem], 1)

            def sequence(i, stage_name, n, sem, name, c0, src, rows, b, mode):
                free(i, stage_name, n, mode)
                product(bank(stage_name, n)[:, 0:D], a_tiles(src, rows, b * T, T), w_tiles(name, rows, c0, D)) \
                    .then_inc(S[sem], 1)

            def transpose_norm(i, n, b, mode):
                if n or not b:
                    free(i, "xhatT", 2 * n + b, mode)
                pe.wait_ge(S["xhat_ready"], norm_at("xhat_ready", i, n, b, mode))
                src = x0_hat if n == 0 else xhat
                for k in range(KT):
                    c = (k * PAIR + b) * T if n == 0 else k * T
                    t = nc.tensor.transpose(bank("xhatT", 2 * n + b if n else 0)[:, c:c + T],
                                            src[:, b, k * P:(k + 1) * P], ident[:])
                t.then_inc(S["xhatT_ready"], 1)

            def transpose_context(i, j, mode):
                free(i, "cT", 0, mode)
                pe.wait_ge(S["c_loaded"], at("c_loaded", j, 16))
                for b in range(PAIR):
                    for k in range(2):
                        m = nc.tensor.transpose(bank("cT")[0:CK[k], k * TOK + b * T:k * TOK + (b + 1) * T],
                                                c_in[:, b, k * P:k * P + CK[k]], ident[:])
                m.then_inc(S["cT_ready"], 1)

            def keys0(i, n, mode):
                feature_major(i, "k0", n, "k0_ready", "wk", 2 * P * n, (c_h, c_l), CK, mode)

            def values0(i, n, mode):
                free(i, "v0", n, mode)
                product(bank("v0", n)[:], a_tiles((c_h, c_l), CK, (n // 2) * T, T),
                        w_tiles("wv", CK, 512 * (n % 2), 512)).then_inc(S["v0_ready"], 1)

            def queries(i, att, b, mode):
                n = 2 * (att - 1) + b
                free(i, "qk", n, mode)
                pe.wait_ge(S["h_full"], norm_at("h_full", i, att, b, mode))
                w = wqk if att == 1 else wq2
                for t in range(2 * T1 if att == 1 else T1):
                    for k in range(KT):
                        m = nc.tensor.matmul(bank("qk", n)[:, t * T:(t + 1) * T], w[:, k, t * P:(t + 1) * P],
                                             h_f[:, k, b * T:(b + 1) * T], start=(k == 0), stop=(k == KT - 1))
                m.then_inc(S["qk_ready"], 1)

            def values(i, b, mode):
                pe.wait_ge(S["h_lo"], norm_at("h_lo", i, 1, b, mode))
                sequence(i, "v1", b, "v1_ready", "v1", 0, (h_h, h_l), FULL, b, mode)

            def attended(i, att, b, mode):
                n = 2 * att + b
                if att == 0:
                    pe.wait_ge(S["oT_lo"], at("oT_lo", i, 4 * b + 4))
                    sequence(i, "resid", n, "resid_ready", "wo", 0, (oT_h, oT_l), [P] * T0, b, mode)
                else:
                    pe.wait_ge(S["oT_lo"], at("oT_lo", i, GROUPS + n - 1))
                    sequence(i, "resid", n, "resid_ready", "mid", MIDCOL["pr" if att == 1 else "ou"],
                             (o1T_h, o1T_l), FULL, b, mode)

            def score(i, att, g):
                n = att * GROUPS + g
                b = g // 4
                dst = sc[n % 3]
                tok = slice(b * T, (b + 1) * T)
                if att == 0:
                    if g in (0, 2):
                        pe.wait_ge(S["q0_done"], at("q0_done", i, g + 2))
                    for j in range(4):
                        h = head0(g, j)
                        r = slice(HD0 * (h % 2), HD0 * (h % 2) + HD0)
                        m = nc.tensor.matmul(dst[:, j, :], q0[r, h // 2, tok], k0[r, h // 2, tok], start=True, stop=True)
                else:
                    pe.wait_ge(S["q_split" if g % 4 < 2 else "q_split_late"],
                               at("q_split", i, 4 * (att - 1) + 2 * b + g % 2 + 1))
                    if att == 1 and g % 4 == 0:
                        pe.wait_ge(S["k1_done"], at("k1_done", i, b + 1))
                    keys = k1 if att == 1 else k2
                    nc.tensor.matmul(dst[:], identb[:], mask_add[:, att - 1, b:b + 1, :].to_broadcast([P, 4, T]),
                                     start=True, stop=False)
                    for j in range(4):
                        t, h = divmod(head1(g, j), H // T1)
                        m = nc.tensor.matmul(dst[:, j, :], q1[:, b, t, h, :], keys[:, t, tok], start=False, stop=(j == 3))
                m.then_inc(S["scores_ready"], 1)

            def turn_probs(i, att, g):
                n = att * GROUPS + g
                pe.wait_ge(S["exp_done"], at("exp_done", i, n + 1))
                for j in range(4):
                    m = nc.tensor.transpose(pt[g % 2][:, j, :], probs[:, g % 3, j, :], ident[:])
                m.then_inc(S["pt_ready"], 1)

            def weigh(i, att, g, mode):
                n, b = att * GROUPS + g, g // 4
                if att == 0:
                    free(i, "pv0", g, mode)
                elif g % 4 == 0:
                    free(i, f"pv{att}", b, mode)
                if att == 1 and g % 4 == 0:
                    pe.wait_ge(S["v1_done"], at("v1_done", i, b + 1))
                if att == 2 and g == 0:
                    pe.wait_ge(S["v1_done"], at("v1_done", i, 3))
                pe.wait_ge(S["pts_ready"], at("pts_ready", i, n + 1))
                for j in range(4):
                    if att == 0:
                        dst = bank("pv0", g)[:, j * (HD0 + 1):(j + 1) * (HD0 + 1)]
                        v = v0[:, b, head0(g, j), :]
                    else:
                        h = head1(g, j)
                        dst = bank(f"pv{att}", b)[:, h * (HD1 + 1):(h + 1) * (HD1 + 1)]
                        v = (v1 if att == 1 else v2)[:, b, h, :]
                    m = nc.tensor.matmul(dst, pts[:, g % 2, j, :], v, start=True, stop=True)
                m.then_inc(S["pv_done"], 1)

            def turn_out0(i, g, mode):
                free(i, "oT0", g, mode)
                pe.wait_ge(S["on_ready"], at("on_ready", i, g + 1))
                for k in range(2):
                    m = nc.tensor.transpose(bank("oT0", g)[:, k * P:(k + 1) * P], o_n[:, g % 2, k * P:(k + 1) * P],
                                            ident[:])
                m.then_inc(S["oT_ready"], 1)

            def turn_out1(i, att, b, mode):
                free(i, f"oT{att}", b, mode)
                pe.wait_ge(S["on_ready"], at("on_ready", i, GROUPS + 2 * att - 1 + b))
                for k in range(T1):
                    m = nc.tensor.transpose(bank(f"oT{att}", b)[:, k * T:(k + 1) * T], o_n[:, b, k * P:(k + 1) * P],
                                            ident[:])
                m.then_inc(S["oT_ready"], 1)

            def values2(i, mode):
                free(i, "v2", 0, mode)
                for b in range(PAIR):
                    m = product(bank("v2")[:, b * D:(b + 1) * D], a_tiles((c_h, c_l), CK, b * T, T),
                                w_tiles("mid", CK, MIDCOL["v2"], D))
                m.then_inc(S["v1_ready"], 1)

            def turn(i, mode):
                used[0] = 0
                pe.wait_ge(S["k0_done"], at("k0_done", i, 4))
                pe.wait_ge(S["v0_done"], at("v0_done", i, 4))
                pe.wait_ge(S["h_lo"], PER["h_lo"] * i + PAIR)
                for n in range(4):
                    if n in (1, 2):
                        pe.wait_ge(S["resid_done"], at("resid_done", i, n - 2))
                    if n == 3:
                        score(i, 0, 0)
                    feature_major(i, "q0", n, "q0_ready", "wq", 2 * P * n, (x0_h, x0_l), FULL, mode)
                for s in range(GROUPS + LAG_O):
                    if 0 < s < GROUPS:
                        score(i, 0, s)
                    if s == GROUPS + LAG_O - 1:
                        queries(i, 1, 0, mode)
                    if LAG_O <= s < GROUPS:
                        turn_out0(i, s - LAG_O, mode)
                    if s == 8:
                        attended(i, 0, 0, mode)
                    if s == 10:
                        transpose_norm(i, 1, 0, mode)
                    if 0 <= s - LAG_T < GROUPS:
                        turn_probs(i, 0, s - LAG_T)
                    if 0 <= s - LAG_PV < GROUPS:
                        weigh(i, 0, s - LAG_PV, mode)
                    if s >= GROUPS:
                        turn_out0(i, s - LAG_O, mode)
                values(i, 0, mode)
                attended(i, 0, 1, mode)
                pe.wait_ge(S["masks_ready"], at("masks_ready", i, 2))
                for att in (1, 2):
                    for s in range(GROUPS + LAG_PV):
                        if s < GROUPS:
                            score(i, att, s)
                        if s == 2 and att == 1:
                            transpose_norm(i, att, 1, mode)
                        if s == 3:
                            queries(i, att, 1, mode)
                        if s == 0 and att == 2:
                            attended(i, 1, 1, mode)
                        if s == 7:
                            turn_out1(i, att, 0, mode)
                        if 0 <= s - LAG_T < GROUPS:
                            turn_probs(i, att, s - LAG_T)
                        if s == 2 and att == 2:
                            transpose_norm(i, att, 1, mode)
                        if s == 8:
                            attended(i, att, 0, mode)
                        if 0 <= s - LAG_PV < GROUPS:
                            weigh(i, att, s - LAG_PV, mode)
                        if s == 3 and att == 1:
                            values(i, 1, mode)
                        if s == 3 and att == 2 and mode == MORE:
                            transpose_context(i, i + 1, mode)
                        if s == 6 and att == 2 and mode == MORE:
                            transpose_norm(i, 0, 0, mode)
                            transpose_norm(i, 0, 1, mode)
                        if s == 8:
                            if att == 1:
                                feature_major(i, "k2", 0, "k2_ready", "mid", MIDCOL["k2"], (c_h, c_l), CK, mode)
                            elif mode == MORE:
                                pe.wait_ge(S["c_lo"], at("c_lo", i + 1, 2))
                                keys0(i, 0, mode)
                        if s == 9:
                            transpose_norm(i, att + 1, 0, mode)
                        if s == 10:
                            if att == 1:
                                queries(i, 2, 0, mode)
                            elif mode == MORE:
                                keys0(i, 1, mode)
                    turn_out1(i, att, 1, mode)
                    if att == 1:
                        values2(i, mode)
                        pe.wait_ge(S["k2_done"], at("k2_done", i, 1))
                if mode == MORE:
                    keys0(i, 2, mode)
                    keys0(i, 3, mode)
                attended(i, 2, 1, mode)
                if mode == MORE:
                    values0(i, 0, mode)
                    values0(i, 1, mode)
                transpose_norm(i, 3, 1, mode)
                if mode == MORE:
                    values0(i, 2, mode)
                    values0(i, 3, mode)
                pe.wait_ge(S["h_lo"], norm_at("h_lo", i, 3, 1, mode))
                for n in range(4):
                    feature_major(i, "up", n, "up_ready", "up", 2 * P * n, (h_h, h_l), FULL, mode)
                free(i, "resid", 6, mode)
                free(i, "resid", 7, mode)
                for n in range(4):
                    pe.wait_ge(S["g_lo"], at("g_lo", i, n + 1))
                    for b in range(PAIR):
                        m = product(bank("resid", 6 + b)[:, 0:D],
                                    [(g_h[:, k, b * T:(b + 1) * T], g_l[:, k, b * T:(b + 1) * T])
                                     for k in (2 * n, 2 * n + 1)],
                                    [(W["down"][0][:, k, :], W["down"][1][:, k, :]) for k in (2 * n, 2 * n + 1)],
                                    first=(n == 0), last=(n == 3))
                        if n == 3:
                            m.then_inc(S["resid_ready"], 1)

            pe.wait_ge(S["consts_built"], 8)
            transpose_context(0, 0, PRE)
            pe.wait_ge(S["params_loaded"], 16 * (len(COL) + len(BROWS)))
            nc.tensor.transpose(sc[0][:, 0, 0:at_col], prow[0:at_col, :], ident[0:at_col, 0:at_col]) \
                .then_inc(S["params_turned"], 1)
            pe.wait_ge(S["w_lo_done"], NPIECE[-1])
            pe.wait_ge(S["prepared"], 1)
            pe.wait_ge(S["raw_loaded"], 32)
            transpose_norm(0, 0, 0, PRE)
            transpose_norm(0, 0, 1, PRE)
            pe.wait_ge(S["c_lo"], at("c_lo", 0, 2))
            for n in range(4):
                keys0(0, n, PRE)
            for n in range(4):
                values0(0, n, PRE)
            with pe.Fori(0, TURNS - 1) as i:
                turn(i, MORE)
            turn(TURNS - 1, LAST)


_OUT = ((32, 128, 256), 'float32')


def kernel(**inputs):
    import numpy as _np
    import concourse.bacc as _bacc
    from concourse import mybir as _mybir
    from concourse.bass_utils import run_bass_kernel_spmd as _run

    nc = _bacc.Bacc("TRN2", target_bir_lowering=False, num_devices=1)
    arrays, args = {}, {}
    for name, value in inputs.items():
        x = _np.ascontiguousarray(value)
        arrays[f"in_{name}_dram"] = x
        args[name] = nc.dram_tensor(f"in_{name}_dram", x.shape, _mybir.dt.from_np(x.dtype), kind="ExternalInput").ap()
    out = nc.dram_tensor("out_0_dram", _OUT[0], _mybir.dt.float32, kind="ExternalOutput").ap()
    decoder_kernel(nc, args, out)
    r = _run(nc, [arrays], core_ids=[0])
    return r.results[0]["out_0_dram"]
```
